# Optimizing a Trainium2 kernel written in Bass

```python
import numpy as np
import jax
import jax.numpy as jnp

def _softmax(x, axis=-1):
    return jax.nn.softmax(x, axis=axis)

def _gelu(x):
    return jax.nn.gelu(x, approximate=True)

def _silu(x):
    return jax.nn.silu(x)

def _sigmoid(x):
    return jax.nn.sigmoid(x)

def _layernorm(x, axis=-1, eps=1e-05):
    m = jnp.mean(x, axis=axis, keepdims=True)
    v = jnp.var(x, axis=axis, keepdims=True)
    return (x - m) / jnp.sqrt(v + eps)

def _scatter_add(tgt, idx, src, axis=0):
    return tgt.at[idx].add(src)

def _segment_sum(src, seg, n):
    return jax.ops.segment_sum(src, seg, n)
kernel_name = 'mk_decoder_preln_d1_seqx_r8_fc4bb7'

def setup_inputs(seed: int=0):
    np.random.seed(seed)
    _w = jnp.asarray

    def _rec_inputs():
        import jax
        import jax.numpy as jnp
        _rk = jax.random.key(seed)
        x = 0.0002417 + 0.9998 * jax.random.normal(jax.random.fold_in(_rk, 1), (32, 128, 128), jnp.float32)
        _lenS = 128 - jax.random.randint(jax.random.fold_in(_rk, 7), (32,), 0, max(1, 128 // 4) + 1, jnp.int32)
        _lenS2 = 77 - jax.random.randint(jax.random.fold_in(_rk, 8), (32,), 0, max(1, 77 // 4) + 1, jnp.int32)
        _ctx_1024P = jax.random.normal(jax.random.fold_in(_rk, 11), (32, 16, 128), jnp.float32)
        _ctx_1024c = jax.random.dirichlet(jax.random.fold_in(_rk, 511), 0.3 * jnp.ones((16,), jnp.float32), (32, 77))
        _ctx_1024t = jnp.einsum('bsk,bkd->bsd', _ctx_1024c, _ctx_1024P)
        _ctx_1024t = _ctx_1024t * jax.lax.rsqrt(jnp.mean(jnp.square(_ctx_1024t)) + 1e-12) * 0.953939
        ctx_1024 = 7.22013e-05 + 1.00017 * (_ctx_1024t + 0.3 * jax.random.normal(jax.random.fold_in(_rk, 611), (32, 77, 128), jnp.float32))
        return (x, ctx_1024)
    x, ctx_1024 = _rec_inputs()

    def _L0_attn_setup():
        import jax, jax.numpy as jnp
        import numpy as np
        FEATS = 128
        HEAD = 16
        HEAD_DIM = FEATS // HEAD
        EPS = 1e-12

        def _l2norm(t):
            n = jnp.sqrt(jnp.sum(t * t, axis=-1, keepdims=True))
            return t / jnp.maximum(n, EPS)
        key = jax.random.key(seed)
        ks = jax.random.split(key, 10)
        s = 0.02
        inp = {'x': jax.random.normal(ks[0], (4, 256, FEATS), dtype=jnp.float32), 'Wq': jax.random.normal(ks[1], (FEATS, FEATS), dtype=jnp.float32) * s, 'bq': jnp.zeros((FEATS,), dtype=jnp.float32), 'Wk': jax.random.normal(ks[2], (FEATS, FEATS), dtype=jnp.float32) * s, 'bk': jnp.zeros((FEATS,), dtype=jnp.float32), 'Wv': jax.random.normal(ks[3], (FEATS, FEATS), dtype=jnp.float32) * s, 'bv': jnp.zeros((FEATS,), dtype=jnp.float32), 'Wo': jax.random.normal(ks[4], (FEATS, FEATS), dtype=jnp.float32) * s, 'bo': jnp.zeros((FEATS,), dtype=jnp.float32), 'm': jnp.full((HEAD,), 0.5, dtype=jnp.float32)}
        return inp
    _L0_attn_all = _L0_attn_setup()
    _L0_attn_in = {k: v for k, v in _L0_attn_all.items() if k in ('Wq', 'bq', 'Wk', 'bk', 'Wv', 'bv', 'Wo', 'bo', 'm')}
    del _L0_attn_all

    def _L0_xattn_setup():
        import jax, jax.numpy as jnp
        import numpy as np
        EMBED = 128
        HEADS = 16
        HEAD_DIM = EMBED // HEADS
        EXP_DIM = 2 * HEAD_DIM

        def _feature_map(x, fm_w, fm_b):
            z = jnp.einsum('nshd,ed->nshe', x, fm_w) + fm_b
            return jnp.concatenate([jnp.exp(z), jnp.exp(-z)], axis=-1)
        key = jax.random.key(seed)
        ks = jax.random.split(key, 7)
        N, S = (4, 256)
        values = jax.random.normal(ks[0], (N, S, EMBED), dtype=jnp.float32)
        keys_ = jax.random.normal(ks[1], (N, S, EMBED), dtype=jnp.float32)
        query = jax.random.normal(ks[2], (N, S, EMBED), dtype=jnp.float32)
        fm_w = jnp.eye(HEAD_DIM, dtype=jnp.float32) + 0.02 * jax.random.normal(ks[3], (HEAD_DIM, HEAD_DIM), dtype=jnp.float32)
        fm_b = 0.02 * jax.random.normal(ks[4], (HEAD_DIM,), dtype=jnp.float32)
        fc_w = jax.random.normal(ks[5], (EMBED, HEADS * EXP_DIM), dtype=jnp.float32) * (1.0 / np.sqrt(HEADS * EXP_DIM))
        fc_b = jnp.zeros((EMBED,), dtype=jnp.float32)
        return {'values': values, 'keys': keys_, 'query': query, 'fm_w': fm_w, 'fm_b': fm_b, 'fc_w': fc_w, 'fc_b': fc_b}
    _L0_xattn_all = _L0_xattn_setup()
    _L0_xattn_in = {k: v for k, v in _L0_xattn_all.items() if k in ('fm_w', 'fm_b', 'fc_w', 'fc_b')}
    del _L0_xattn_all

    def _L0_ffn_setup():
        import jax, jax.numpy as jnp
        import numpy as np
        B, S, H = (2, 256, 128)
        N, F, SF, K = (16, 128, 512, 1)
        key = jax.random.key(seed)
        ks = jax.random.split(key, 7)
        std = 0.02
        return {'hidden_states': jax.random.normal(ks[0], (B, S, H), dtype=jnp.float32), 'router_w': jax.random.normal(ks[1], (N, H), dtype=jnp.float32) * std, 'gate_up_proj': jax.random.normal(ks[2], (N, H, 2 * F), dtype=jnp.float32) * std, 'down_proj': jax.random.normal(ks[3], (N, F, H), dtype=jnp.float32) * std, 'shared_gate_w': jax.random.normal(ks[4], (SF, H), dtype=jnp.float32) * std, 'shared_up_w': jax.random.normal(ks[5], (SF, H), dtype=jnp.float32) * std, 'shared_down_w': jax.random.normal(ks[6], (H, SF), dtype=jnp.float32) * std}
    _L0_ffn_all = _L0_ffn_setup()
    _L0_ffn_in = {k: v for k, v in _L0_ffn_all.items() if k in ('router_w', 'gate_up_proj', 'down_proj', 'shared_gate_w', 'shared_up_w', 'shared_down_w')}
    del _L0_ffn_all
    return {'x': x, 'ctx_1024': ctx_1024, 'L0_attn_Wq': _L0_attn_in['Wq'], 'L0_attn_bq': _L0_attn_in['bq'], 'L0_attn_Wk': _L0_attn_in['Wk'], 'L0_attn_bk': _L0_attn_in['bk'], 'L0_attn_Wv': _L0_attn_in['Wv'], 'L0_attn_bv': _L0_attn_in['bv'], 'L0_attn_Wo': _L0_attn_in['Wo'], 'L0_attn_bo': _L0_attn_in['bo'], 'L0_attn_m': _L0_attn_in['m'], 'L0_xattn_fm_w': _L0_xattn_in['fm_w'], 'L0_xattn_fm_b': _L0_xattn_in['fm_b'], 'L0_xattn_fc_w': _L0_xattn_in['fc_w'], 'L0_xattn_fc_b': _L0_xattn_in['fc_b'], 'L0_ffn_router_w': _L0_ffn_in['router_w'], 'L0_ffn_gate_up_proj': _L0_ffn_in['gate_up_proj'], 'L0_ffn_down_proj': _L0_ffn_in['down_proj'], 'L0_ffn_shared_gate_w': _L0_ffn_in['shared_gate_w'], 'L0_ffn_shared_up_w': _L0_ffn_in['shared_up_w'], 'L0_ffn_shared_down_w': _L0_ffn_in['shared_down_w']}

def reference(x, ctx_1024, L0_attn_Wq, L0_attn_bq, L0_attn_Wk, L0_attn_bk, L0_attn_Wv, L0_attn_bv, L0_attn_Wo, L0_attn_bo, L0_attn_m, L0_xattn_fm_w, L0_xattn_fm_b, L0_xattn_fc_w, L0_xattn_fc_b, L0_ffn_router_w, L0_ffn_gate_up_proj, L0_ffn_down_proj, L0_ffn_shared_gate_w, L0_ffn_shared_up_w, L0_ffn_shared_down_w):
    import jax
    import jax.numpy as jnp

    def _L0_attn_ref(x, Wq, bq, Wk, bk, Wv, bv, Wo, bo, m):
        import jax, jax.numpy as jnp
        import numpy as np
        FEATS = 128
        HEAD = 16
        HEAD_DIM = FEATS // HEAD
        EPS = 1e-12

        def _l2norm(t):
            n = jnp.sqrt(jnp.sum(t * t, axis=-1, keepdims=True))
            return t / jnp.maximum(n, EPS)
        b, n, f = x.shape

        def proj(W, bias):
            y = x @ W + bias
            return y.reshape(b, n, HEAD, HEAD_DIM).transpose(0, 2, 1, 3)
        q = _l2norm(proj(Wq, bq))
        k = _l2norm(proj(Wk, bk))
        v = proj(Wv, bv)
        sim = jnp.einsum('bhid,bhjd->bhij', q, k)
        sigma_m = jax.nn.sigmoid(m).reshape(1, HEAD, 1, 1)
        scaling = jnp.asarray(n, dtype=x.dtype) ** sigma_m
        attn = sim / scaling
        out = jnp.einsum('bhij,bhjd->bhid', attn, v)
        out = out.transpose(0, 2, 1, 3).reshape(b, n, f)
        return out @ Wo + bo

    def _L0_xattn_ref(values, keys, query, fm_w, fm_b, fc_w, fc_b):
        import jax, jax.numpy as jnp
        import numpy as np
        EMBED = 128
        HEADS = 16
        HEAD_DIM = EMBED // HEADS
        EXP_DIM = 2 * HEAD_DIM

        def _feature_map(x, fm_w, fm_b):
            z = jnp.einsum('nshd,ed->nshe', x, fm_w) + fm_b
            return jnp.concatenate([jnp.exp(z), jnp.exp(-z)], axis=-1)
        N, S, _ = query.shape
        v = values.reshape(N, -1, HEADS, HEAD_DIM)
        k = keys.reshape(N, -1, HEADS, HEAD_DIM)
        q = query.reshape(N, -1, HEADS, HEAD_DIM)
        v, k, q = (_feature_map(x, fm_w, fm_b) for x in (v, k, q))
        scores = jnp.einsum('nqhd,nkhd->nhqk', q, k) / jnp.sqrt(jnp.float32(EMBED))
        attn = jax.nn.softmax(scores, axis=-1)
        out = jnp.einsum('nhql,nlhd->nqhd', attn, v)
        out = out.reshape(N, S, HEADS * EXP_DIM)
        return out @ fc_w.T + fc_b

    def _L0_ffn_ref(hidden_states, router_w, gate_up_proj, down_proj, shared_gate_w, shared_up_w, shared_down_w):
        import jax, jax.numpy as jnp
        import numpy as np
        B, S, H = (2, 256, 128)
        N, F, SF, K = (16, 128, 512, 1)
        b, s, h = hidden_states.shape
        hidden = hidden_states.reshape(-1, h)
        t = hidden.shape[0]
        logits = hidden @ router_w.T
        top_vals, top_idx = jax.lax.top_k(logits, K)
        scores = jnp.full_like(logits, -jnp.inf)
        scores = scores.at[jnp.arange(t)[:, None], top_idx].set(top_vals)
        scores = jax.nn.sigmoid(scores.astype(jnp.float32)).astype(hidden.dtype)
        routed_in = hidden[None, :, :] * scores.T[:, :, None]
        gate_up = jnp.einsum('nth,nhf->ntf', routed_in, gate_up_proj)
        gate, up = jnp.split(gate_up, 2, axis=-1)
        routed_out = jnp.einsum('ntf,nfh->nth', up * jax.nn.silu(gate), down_proj)
        expert_sum = routed_out.sum(axis=0)
        shared = jax.nn.silu(hidden @ shared_gate_w.T) * (hidden @ shared_up_w.T) @ shared_down_w.T
        return (shared + expert_sum).reshape(b, s, h)
    x = x + _L0_attn_ref(_layernorm(x, axis=-1), L0_attn_Wq, L0_attn_bq, L0_attn_Wk, L0_attn_bk, L0_attn_Wv, L0_attn_bv, L0_attn_Wo, L0_attn_bo, L0_attn_m)
    x = x + _L0_xattn_ref(ctx_1024, ctx_1024, _layernorm(x, axis=-1), L0_xattn_fm_w, L0_xattn_fm_b, L0_xattn_fc_w, L0_xattn_fc_b)
    x = x + _L0_ffn_ref(_layernorm(x, axis=-1), L0_ffn_router_w, L0_ffn_gate_up_proj, L0_ffn_down_proj, L0_ffn_shared_gate_w, L0_ffn_shared_up_w, L0_ffn_shared_down_w)
    return x

_drawn_inputs = setup_inputs


def setup_inputs(seed=0):
    import zlib

    import numpy as np

    out = dict(_drawn_inputs(seed))
    spreads = {'L0_attn_bq': (0.0, 0.742),
     'L0_attn_bk': (0.0, 0.4),
     'L0_attn_bv': (0.0, 0.411),
     'L0_attn_bo': (0.0, 0.1),
     'L0_attn_m': (0.5, 0.6),
     'L0_xattn_fc_b': (0.0, 0.8)}
    factors = {'L0_attn_Wk': 3.65,
     'L0_attn_Wv': 4.106,
     'L0_ffn_router_w': 8.0,
     'L0_ffn_gate_up_proj': 8.0,
     'L0_ffn_down_proj': 8.0,
     'L0_ffn_shared_gate_w': 8.0,
     'L0_ffn_shared_up_w': 8.0,
     'L0_ffn_shared_down_w': 8.0}
    for name, (base, spread) in spreads.items():
        noise = np.random.default_rng([zlib.crc32(name.encode()), seed]).standard_normal(out[name].shape)
        drawn = base * np.exp(spread * noise) if base else spread * noise
        out[name] = jnp.asarray(drawn.astype(out[name].dtype))
    for name, factor in factors.items():
        out[name] = (out[name] * factor).astype(out[name].dtype)
    return out
```

```python
import math
from contextlib import ExitStack

import concourse.bass as bass
from concourse import mybir

ALU = mybir.AluOpType
ACT = mybir.ActivationFunctionType
AX = mybir.AxisListType
F32 = mybir.dt.float32
BF16 = mybir.dt.bfloat16
I32 = mybir.dt.int32
U32 = mybir.dt.uint32

P = 128
HEADS, HD = 16, 8
EX = 2 * HD
HALF = HEADS // 2
LN_EPS, L2_EPS = 1e-5, 1e-12
PARTS = 3
Q_PART = (0, 0, 0, 1, 1, 2)
K_PART = (0, 1, 2, 0, 1, 0)
ROWS = len(Q_PART) * EX
SHIFT_ROWS = ROWS + PARTS


def decoder_layer(nc, t, out):
    B, S, D = t["x"].shape
    KEYS = t["ctx_1024"].shape[1]
    EXPERTS, _, FF2 = t["L0_ffn_gate_up_proj"].shape
    FF = FF2 // 2
    SF = t["shared_gateT"].shape[1]
    CH = SF // P
    TOK = B * S
    JP = 4
    NG = B // JP
    GT = JP * S
    JK = JP * KEYS
    JA = 2
    NA = B // JA
    NBUF = 4
    TILES = TOK // P + EXPERTS
    SLOTS = TILES * P
    ROW = D + 4
    assert S == D == P and FF == P and HEADS * HD == D and GT == 512
    SCORE_SCALE = float(D) ** -0.5
    UNITS = ((0, 6), (6, 11), (11, 16))

    with ExitStack() as ctx:
        def sb(name, shape, dt=F32):
            return ctx.enter_context(nc.sbuf_tensor(name, shape, dt))

        def arena(name, size):
            start = nc.sbuf_base
            ctx.enter_context(nc.sbuf_tensor(name, [P, size // 4], F32))

            def phase():
                at = [start]

                def place(n, shape, dt=F32):
                    tile = nc.alloc_sbuf_tensor_at(n, shape, dt, offset=at[0])
                    words = 1
                    for d in shape[1:]:
                        words *= d
                    at[0] += -(-words * mybir.dt.size(dt) // 32) * 32
                    assert at[0] <= start + size, (n, at[0] - start)
                    return tile
                return place
            return phase

        def sem(name):
            return ctx.enter_context(nc.semaphore(name))

        bank = [ctx.enter_context(nc.psum_tensor(f"bank{i}", [P, 512], F32)) for i in range(8)]

        qparts = nc.dram_tensor("qparts", (2, P, PARTS, TOK), BF16).ap()
        kparts = nc.dram_tensor("kparts", (2, P, PARTS, B * KEYS), BF16).ap()
        sorted_in = nc.dram_tensor("sorted_in", (SLOTS, ROW), F32).ap()
        routed = nc.dram_tensor("routed", (TOK + SLOTS, D), F32).ap()

        ident = sb("ident_s", [P, P])
        ident_b = sb("ident_b", [P, P], BF16)
        headmask = sb("headmask_s", [P, P])
        signs = sb("signs_s", [P, 2, P])
        signcol = sb("signcol_s", [P, 1])
        before_f = sb("before_f", [P, P])
        before = sb("before_b", [P, P], BF16)
        ones_b = sb("ones_b", [P, P], BF16)
        expert_no = sb("expert_no", [P, EXPERTS])
        tile_no = sb("tile_no", [P, TILES])
        token_no = sb("token_no", [P, B], I32)
        slot_no = sb("slot_no_s", [P, TILES], I32)
        wqkv = sb("wqkv", [P, 3 * D])
        bqkv = sb("bqkv", [P, 3 * D])
        wo = sb("wo", [P, D])
        bo = sb("bo", [P, D])
        m_col = sb("m_col", [P, 1])
        inv_scale = sb("inv_scale", [P, 4])
        map_w = sb("map_w", [P, 2, P])
        map_b = sb("map_b", [P, 2])
        fcw = sb("fcw", [P, 2, D])
        fcb = sb("fcb", [P, D])
        rw = sb("rw", [P, EXPERTS])
        sg = sb("sg", [P, SF])
        su = sb("su", [P, SF])
        sd = sb("sd", [P, CH, D])
        eps = sb("eps", [P, 1])
        eps_p = sb("eps_p", [P, 1])
        carrier_p = sb("carrier_p", [P, 1])
        carrier = sb("carrier", [P, 1])

        xs = sb("xs", [P, B, D])
        xT = sb("xT", [P, TOK])
        vals = sb("vals", [KEYS, B, HEADS, EX + 1])
        stats = sb("stats", [P, JP, 6])
        stats3 = sb("stats3", [P, B, 6])
        mv = sb("mv", [P, B, 2])
        std = sb("std", [P, B])
        rstd = sb("rstd", [P, B])
        xn = [sb(f"xn{i}", [P, JP, D]) for i in range(2)]

        s = {}
        for n in ("const_in", "weights_in", "fill_set", "carried", "filled", "sentinels", "cast", "map_ready", "esc", "esc_dve", "inv_ready",
                  "stat1", "mean1", "std1", "rstd1", "xn1", "xT1p", "xT1", "qkvp", "qkv1", "sq1", "ss1", "nrm1",
                  "nmax1", "rn1", "qkn1", "qTp", "qT1", "kvp", "mt1", "mwp", "mw1", "yp", "xb1", "x1",
                  "stat2", "mean2", "std2", "rstd2", "xn2", "xT2p", "xT2",
                  "zqp", "qf", "qhi", "qres", "qmid", "qlo", "q_out", "ctxTp", "ctxT", "zkp", "kf", "khi", "kres",
                  "kmid", "klo", "k_out", "vp", "v_ready", "q_last", "k_last",
                  "ap", "amax", "neg", "mhi", "mres", "mmid", "mlo", "mTp", "mT", "bp", "expd", "avp", "avs",
                  "ones_rows", "set", "v_cur", "tavp", "rden", "avn", "t2p", "t2", "fcp", "x2", "stat3", "mean3", "xb2",
                                    "std3", "rstd3", "xn3", "h_kept", "hTp", "hT", "lgp", "lgT", "lgtp", "lg",
                  "r_step", "oh", "rankp", "escore", "score", "sc_ready", "pos", "rows", "scat", "etile",
                  "gup", "silu", "act", "downp", "x3",
                  "tin", "tTp", "tT", "tgup", "tsilu", "tact", "tyd", "ty", "tout", "res_in", "res_add", "res_out"):
            s[n] = sem(n)
        x_in = [sem(f"x_in{i}") for i in range(2)]
        c_in = [sem(f"c_in{i}") for i in range(2)]
        q_in = [sem(f"q_in{i}") for i in range(NBUF)]
        k_in = [sem(f"k_in{i}") for i in range(NBUF)]
        m_in = [sem(f"m_in{i}") for i in range(NBUF)]
        q_sent = [sem(f"q_sent{i}") for i in range(2)]
        k_sent = [sem(f"k_sent{i}") for i in range(2)]
        t_in = [sem(f"t_in{i}") for i in range(NBUF)]
        t_out = [sem(f"t_out{i}") for i in range(NBUF)]
        y_in = [sem(f"y_in{i}") for i in range(2)]

        def seqs(tile, g, n=JP):
            return tile[:, bass.ds(g * n, n)]

        def is_first(g):
            return isinstance(g, int) and g == 0

        def wait_on_copy(v, semaphore, value):
            v.wait_ge(semaphore, value)
            v.tensor_copy(carrier[:], eps[:])

        CONSTS = [(ident, "ident"), (headmask, "headmask"), (signs, "signs"), (signcol, "signcol"),
                  (before_f, "before"), (expert_no, "expert_no"), (tile_no, "tile_no"), (token_no, "token_no"), (slot_no, "slot_no"),
                  (map_w, "fm_wT"), (map_b[:, 0:1], "fm_b"), (m_col, "m_col"),
                  (wqkv[:, 0:D], "L0_attn_Wq"), (wqkv[:, D:2 * D], "L0_attn_Wk"), (wqkv[:, 2 * D:3 * D], "L0_attn_Wv"),
                  (wo, "L0_attn_Wo")]
        ROWS_BCAST = [(bqkv[:, 0:D], "L0_attn_bq"), (bqkv[:, D:2 * D], "L0_attn_bk"),
                      (bqkv[:, 2 * D:3 * D], "L0_attn_bv"), (bo[:], "L0_attn_bo"), (fcb[:], "L0_xattn_fc_b")]
        LATE = [(fcw, "fc_wT"), (rw, "router_wT"), (sg, "shared_gateT"), (su, "shared_upT"), (sd, "shared_downT")]

        def ap_of(a):
            return a if isinstance(a, bass.AP) else a[:]

        def sp_phase0(sp):
            sp.dma_start(xs[:, 0:JP], x_seq(0)).then_inc(x_in[0], 16)
            for dst, name in CONSTS:
                sp.dma_start(ap_of(dst), t[name]).then_inc(s["const_in"], 16)
            for dst, name in ROWS_BCAST:
                sp.dma_start(dst, t[name].rearrange("(o f) -> o f", o=1).broadcast_to([P, D])).then_inc(s["const_in"], 16)
        N_CONST = 16 * (len(CONSTS) + len(ROWS_BCAST))

        def dve_phase0(v):
            v.memset(eps[:], LN_EPS)
            v.memset(ones_b[:], 1.0)
            v.memset(vals[:], 1.0).then_inc(s["set"], 1)
            v.wait_ge(s["const_in"], N_CONST)
            v.tensor_copy(ident_b[:], ident[:]).then_inc(s["cast"], 1)
            v.tensor_copy(before[:], before_f[:]).then_inc(s["cast"], 1)
            v.tensor_tensor(map_w[:], map_w[:], signs[:], ALU.mult).then_inc(s["map_ready"], 1)
            v.tensor_tensor(map_b[:, 1:2], map_b[:, 0:1], signcol[:], ALU.mult).then_inc(s["map_ready"], 1)
            v.wait_ge(s["esc"], 1)
            v.tensor_scalar(inv_scale[:, 1:2], inv_scale[:, 0:1], 1.0, None, ALU.add).then_inc(s["esc_dve"], 1)
            v.wait_ge(s["esc_dve"], 1)
            v.reciprocal(inv_scale[:, 2:3], inv_scale[:, 1:2]).then_inc(s["esc_dve"], 1)

        def act_phase0(a):
            a.wait_ge(s["const_in"], N_CONST)
            a.activation(inv_scale[:, 0:1], m_col[:], ACT.Exp, scale=-1.0).then_inc(s["esc"], 1)
            a.wait_ge(s["esc_dve"], 2)
            a.activation(inv_scale[:, 3:4], inv_scale[:, 2:3], ACT.Exp, scale=-math.log(float(S))).then_inc(s["inv_ready"], 1)

        def x_seq(g):
            return t["x"][bass.ds(g * JP, JP)].rearrange("b p f -> p b f")

        qkv = [sb(f"qkv{i}", [P, JP, 3 * D]) for i in range(2)]
        ctx_s = [sb(f"ctx{i}", [KEYS, JP, D]) for i in range(2)]
        early = arena("early", 32768)
        sb1 = early()
        xnT = [sb1(f"xnT{i}", [P, GT]) for i in range(2)]
        sq = sb1("sq", [P, JP, 2 * D])
        ss = sb1("ss", [P, JP * 2 * HEADS])
        nrm = sb1("nrm", [P, JP * 2 * HEADS])
        rn = sb1("rn", [P, JP * 2 * HEADS])
        qT = sb1("qT", [P, GT])
        mt = sb1("mt", [P, GT])
        mw = sb1("mw", [P, GT])
        xn2 = [sb1(f"xn2_{i}", [P, JP, D]) for i in range(2)]

        def sp_phase1(sp):
            sp.dma_start(seqs(xs, 1), x_seq(1)).then_inc(x_in[1], 16)
            with sp.Fori(1, NG // 2) as g2:
                for par in range(2):
                    sp.wait_ge(x_in[par], g2 * 16)
                    sp.dma_start(seqs(xs, g2 * 2 + par), x_seq(g2 * 2 + par)).then_inc(x_in[par], 16)

        def loop1(eng, front, back):
            front(0, 0, 0)
            with eng.Fori(0, NG // 2 - 1) as g2:
                for par in range(2):
                    front(g2 * 2 + par + 1, 1 - par, g2 + (par + 1) // 2)
                    back(g2 * 2 + par, par)
            front(NG - 1, 1, NG // 2 - 1)
            back(NG - 2, 0)
            back(NG - 1, 1)

        def dve_phase1(v):
            def layer_norm(g, stat, mean, std_s, rstd_s, dst, done):
                for j in range(JP):
                    i = v.bn_stats(stats[:, j], xs[:, bass.ds(g * JP + j, 1)].rearrange("p o f -> p (o f)"))
                i.then_inc(s[stat], 1)
                wait_on_copy(v, s[stat], g + 1)
                for j in range(JP):
                    i = v.bn_aggr(mv[:, j], stats[:, j])
                i.then_inc(s[mean], 1)
                v.wait_ge(s[std_s], g + 1)
                v.reciprocal(rstd[:, 0:JP], std[:, 0:JP]).then_inc(s[rstd_s], 1)
                v.wait_ge(s[rstd_s], g + 1)
                for j in range(JP):
                    i = v.tensor_scalar(dst[:, j], xs[:, bass.ds(g * JP + j, 1)].rearrange("p o f -> p (o f)"),
                                        mv[:, j, 0:1], rstd[:, j:j + 1], ALU.subtract, ALU.mult)
                i.then_inc(s[done], 1)

            def front(g, par, g2):
                v.wait_ge(x_in[par], g2 * 16 + 16)
                layer_norm(g, "stat1", "mean1", "std1", "rstd1", xn[par], "xn1")
                for j in range(JP):
                    v.wait_ge(s["qkvp"], g * JP + (j + 1))
                    v.tensor_tensor(qkv[par][:, j], bank[1 + j % 2][:, 0:3 * D], bqkv[:], ALU.add).then_inc(s["qkv1"], 1)

            def back(g, par):
                v.wait_ge(s["sq1"], g + 1)
                v.tensor_reduce(ss[:], sq[:].rearrange("p j (h d) -> p (j h) d", d=HD), AX.X, ALU.add).then_inc(s["ss1"], 1)
                v.wait_ge(s["nrm1"], g + 1)
                v.tensor_scalar(nrm[:], nrm[:], L2_EPS, None, ALU.max).then_inc(s["nmax1"], 1)
                v.wait_ge(s["nmax1"], g + 1)
                v.reciprocal(rn[:], nrm[:]).then_inc(s["rn1"], 1)
                v.wait_ge(s["kvp"], g + 1)
                v.scalar_tensor_tensor(out=mt[:].rearrange("p (j f) -> p j f", j=JP),
                                       in0=bank[4][:].rearrange("p (j f) -> p j f", j=JP), scalar=inv_scale[:, 3:4],
                                       in1=headmask[:].rearrange("p (o f) -> p o f", o=1).broadcast_to([P, JP, P]),
                                       op0=ALU.mult, op1=ALU.mult).then_inc(s["mt1"], 1)
                v.wait_ge(s["yp"], g + 1)
                v.wait_ge(s["xb1"], g + 1)
                x_g = seqs(xs, g).rearrange("p j f -> p (j f)")
                v.tensor_tensor(x_g, bank[6][:], x_g, ALU.add).then_inc(s["x1"], 1)
                wait_on_copy(v, s["x1"], g + 1)
                layer_norm(g, "stat2", "mean2", "std2", "rstd2", xn2[par], "xn2")
            v.wait_ge(s["inv_ready"], 1)
            loop1(v, front, back)

        def act_phase1(a):
            def stdev(g, mean, std_s):
                a.wait_ge(s[mean], g + 1)
                a.activation(std[:, 0:JP], mv[:, 0:JP, 1], ACT.Sqrt, bias=eps[:]).then_inc(s[std_s], 1)

            def front(g, par, g2):
                stdev(g, "mean1", "std1")
                a.wait_ge(s["xT1p"], g + 1)
                a.copy(xnT[par][:], bank[0][:]).then_inc(s["xT1"], 1)

            def back(g, par):
                a.wait_ge(s["qkv1"], g * JP + JP)
                a.activation(sq[:], qkv[par][:, :, 0:2 * D], ACT.Square).then_inc(s["sq1"], 1)
                a.wait_ge(s["ss1"], g + 1)
                a.activation(nrm[:], ss[:], ACT.Sqrt).then_inc(s["nrm1"], 1)
                a.wait_ge(s["qTp"], g + 1)
                a.copy(qT[:], bank[3][:]).then_inc(s["qT1"], 1)
                a.wait_ge(s["mwp"], g + 1)
                a.copy(mw[:], bank[5][:]).then_inc(s["mw1"], 1)
                stdev(g, "mean2", "std2")
                a.wait_ge(s["xT2p"], g + 1)
                a.copy(xT[:, bass.ds(g * GT, GT)], bank[7][:]).then_inc(s["xT2"], 1)
            a.wait_ge(s["set"], 1)
            loop1(a, front, back)

        def pool_phase1(p):
            def front(g, par, g2):
                p.wait_ge(s["xn1"], g + 1)
                p.tensor_tensor(seqs(xs, g), seqs(xs, g),
                                bo[:].rearrange("p (o f) -> p o f", o=1).broadcast_to([P, JP, D]), ALU.add).then_inc(s["xb1"], 1)

            def back(g, par):
                p.wait_ge(s["rn1"], g + 1)
                for j in range(JP):
                    qk = qkv[par][:, j, 0:2 * D].rearrange("p (h d) -> p h d", d=HD)
                    r = rn[:, j * 2 * HEADS:(j + 1) * 2 * HEADS].rearrange("p (h o) -> p h o", o=1).broadcast_to([P, 2 * HEADS, HD])
                    p.tensor_tensor(qk, qk, r, ALU.mult).then_inc(s["qkn1"], 1)
            p.wait_ge(s["const_in"], N_CONST)
            loop1(p, front, back)

        def pe_phase1(pe):
            def front(g, par, g2):
                pe.wait_ge(s["xn1"], g + 1)
                for j in range(JP):
                    i = pe.transpose(bank[0][:, j * P:(j + 1) * P], xn[par][:, j], ident[:])
                i.then_inc(s["xT1p"], 1)
                pe.wait_ge(s["xT1"], g + 1)
                for j in range(JP):
                    if j >= 2 or not (is_first(g)):
                        pe.wait_ge(s["qkv1"], g * JP + (j - 1))
                    pe.matmul(bank[1 + j % 2][:, 0:3 * D], xnT[par][:, j * P:(j + 1) * P], wqkv[:],
                              start=True, stop=True).then_inc(s["qkvp"], 1)

            def back(g, par):
                for j in range(JP):
                    pe.wait_ge(s["qkn1"], g * JP + (j + 1))
                    i = pe.transpose(bank[3][:, j * P:(j + 1) * P], qkv[par][:, j, 0:D], ident[:])
                i.then_inc(s["qTp"], 1)
                for j in range(JP):
                    i = pe.matmul(bank[4][:, j * P:(j + 1) * P], qkv[par][:, j, 2 * D:3 * D], qkv[par][:, j, D:2 * D],
                                  start=True, stop=True)
                i.then_inc(s["kvp"], 1)
                pe.wait_ge(s["mt1"], g + 1)
                for j in range(JP):
                    i = pe.matmul(bank[5][:, j * P:(j + 1) * P], mt[:, j * P:(j + 1) * P], wo[:], start=True, stop=True)
                i.then_inc(s["mwp"], 1)
                pe.wait_ge(s["qT1"], g + 1)
                pe.wait_ge(s["mw1"], g + 1)
                for j in range(JP):
                    i = pe.matmul(bank[6][:, j * P:(j + 1) * P], qT[:, j * P:(j + 1) * P], mw[:, j * P:(j + 1) * P],
                                  start=True, stop=True)
                i.then_inc(s["yp"], 1)
                pe.wait_ge(s["xn2"], g + 1)
                for j in range(JP):
                    i = pe.transpose(bank[7][:, j * P:(j + 1) * P], xn2[par][:, j], ident[:])
                i.then_inc(s["xT2p"], 1)
            pe.wait_ge(s["const_in"], N_CONST)
            loop1(pe, front, back)

        sb2 = early()
        ctxT = sb2("ctxT_s", [P, JK])
        qf = [sb2(f"qf{i}", [P, GT]) for i in range(2)]
        kf = [sb2(f"kf{i}", [P, JK]) for i in range(2)]
        qpart = [sb2(f"qpart{i}", [P, PARTS, GT], BF16) for i in range(2)]
        kpart = [sb2(f"kpart{i}", [P, PARTS, JK], BF16) for i in range(2)]
        res_q = sb2("res_q", [P, GT])
        res_k = sb2("res_k", [P, JK])

        def loop2(eng, body):
            for par in range(2):
                body(par, par, 0)
            with eng.Fori(1, NG // 2) as g2:
                for par in range(2):
                    body(g2 * 2 + par, par, g2)

        def sp_phase2(sp):
            def ctx_load(g, par):
                sp.dma_start(ctx_s[par][:], t["ctx_1024"][bass.ds(g * JP, JP)].rearrange("b p f -> p b f")).then_inc(c_in[par], 16)
            for par in range(2):
                ctx_load(par, par)

            def body(g, par, g2):
                for hf in range(2):
                    sp.wait_ge(s["klo"], g * 2 + (hf + 1))
                    sp.dma_start(kparts[hf, :, :, bass.ds(g * JK, JK)], kpart[hf][:]).then_inc(k_sent[hf], 16)
                for hf in range(2):
                    sp.wait_ge(s["qlo"], g * 2 + (hf + 1))
                    sp.dma_start(qparts[hf, :, :, bass.ds(g * GT, GT)], qpart[hf][:]).then_inc(q_sent[hf], 16)
            with sp.Fori(0, NG // 2 - 1) as g2:
                for par in range(2):
                    body(g2 * 2 + par, par, g2)
                    sp.wait_ge(s["ctxTp"], g2 * 2 + (par + 1))
                    ctx_load(g2 * 2 + par + 2, par)
            for par in range(2):
                body(NG - 2 + par, par, NG // 2 - 1)

        def pe_phase2(pe):
            def body(g, par, g2):
                pe.wait_ge(c_in[par], g2 * 16 + 16)
                for j in range(JP):
                    i = pe.transpose(bank[0][:, j * KEYS:(j + 1) * KEYS], ctx_s[par][:, j], ident[0:KEYS, 0:KEYS])
                i.then_inc(s["ctxTp"], 1)
                pe.wait_ge(s["ctxT"], g + 1)
                for hf in range(2):
                    pe.matmul(bank[1 + hf][:, 0:JK], map_w[:, hf], ctxT[:], start=True, stop=True).then_inc(s["zkp"], 1)
                for hf in range(2):
                    pe.matmul(bank[3 + hf][:], map_w[:, hf], xT[:, bass.ds(g * GT, GT)],
                              start=True, stop=True).then_inc(s["zqp"], 1)
                pe.wait_ge(s["kf"], g * 2 + 2)
                for hf in range(2):
                    for j in range(JP):
                        i = pe.transpose(bank[5 + j // 2][0:KEYS, (j % 2) * 2 * P + hf * P:(j % 2) * 2 * P + (hf + 1) * P],
                                         kf[hf][:, j * KEYS:(j + 1) * KEYS], ident[:])
                i.then_inc(s["vp"], 1)
                pe.wait_ge(s["qf"], g * 2 + 2)
                pe.wait_ge(s["v_ready"], g * 2 + 2)
            pe.wait_ge(s["xT2"], NG)
            loop2(pe, body)

        def act_phase2(a):
            def body(g, par, g2):
                a.wait_ge(s["ctxTp"], g + 1)
                a.copy(ctxT[:], bank[0][:, 0:JK]).then_inc(s["ctxT"], 1)
                for hf in range(2):
                    a.wait_ge(s["zkp"], g * 2 + (hf + 1))
                    if hf == 0 and not is_first(g):
                        a.wait_ge(s["klo"], g * 2)
                    a.activation(kf[hf][:], bank[1 + hf][:, 0:JK], ACT.Exp, bias=map_b[:, 1:2]).then_inc(s["kf"], 1)
                for hf in range(2):
                    a.wait_ge(s["zqp"], g * 2 + (hf + 1))
                    if hf == 0 and not is_first(g):
                        a.wait_ge(s["qlo"], g * 2)
                    a.activation(qf[hf][:], bank[3 + hf][:], ACT.Exp, bias=map_b[:, 1:2]).then_inc(s["qf"], 1)
                a.wait_ge(s["vp"], g + 1)
                for jj in range(2):
                    a.copy(vals[:, bass.ds(g * JP + 2 * jj, 2), :, 0:EX],
                           bank[5 + jj][0:KEYS].rearrange("p (j h e) -> p j h e", j=2, e=EX)).then_inc(s["v_ready"], 1)
            a.wait_ge(s["map_ready"], 2)
            loop2(a, body)

        def dve_phase2(v):
            def split(g, hf, src, dst, sent, names, res):
                f, hi, rest, mid, lo = names
                n = g * 2 + hf
                v.wait_ge(s[f], n + 1)
                if not is_first(g):
                    v.wait_ge(sent, g * 16)
                v.tensor_copy(dst[:, 0], src).then_inc(s[hi], 1)
                v.wait_ge(s[hi], n + 1)
                v.tensor_tensor(res, src, dst[:, 0], ALU.subtract).then_inc(s[rest], 1)
                v.wait_ge(s[rest], n + 1)
                v.tensor_copy(dst[:, 1], res).then_inc(s[mid], 1)
                v.wait_ge(s[mid], n + 1)
                v.tensor_tensor(dst[:, 2], res, dst[:, 1], ALU.subtract).then_inc(s[lo], 1)

            def body(g, par, g2):
                for hf in range(2):
                    split(g, hf, kf[hf][:], kpart[hf], k_sent[hf], ("kf", "khi", "kres", "kmid", "klo"), res_k[:])
                for hf in range(2):
                    split(g, hf, qf[hf][:], qpart[hf], q_sent[hf], ("qf", "qhi", "qres", "qmid", "qlo"), res_q[:])
            loop2(v, body)

        late = arena("late", 72704)
        sb3 = late()
        qst = [sb3(f"qst{i}", [SHIFT_ROWS, HEADS, JA * S], BF16) for i in range(NBUF)]
        kst = [sb3(f"kst{i}", [SHIFT_ROWS, HEADS, JA * KEYS], BF16) for i in range(NBUF)]
        mx = sb3("mx", [P, JA, HEADS])
        mres = sb3("mres_s", [P, JA, HEADS])
        mpart = sb3("mpart", [P, JA, PARTS + 1, HEADS], BF16)
        mT = [sb3(f"mT{i}", [P, S], BF16) for i in range(2)]
        prob = [sb3(f"prob{i}", [KEYS, 4, S]) for i in range(3)]
        avs = sb3("avs_s", [P, 512])
        rden = sb3("rden_s", [P, HEADS])
        avn = sb3("avn_s", [P, HEADS, EX])
        avnT = sb3("avnT", [P, 2 * P])
        vcur = [sb3(f"vcur{i}", [KEYS, HEADS, EX + 1]) for i in range(2 * JA)]

        def loop3(eng, body, step_a):
            step_a(0, 0, 0)
            step_a(1, 1, 0)
            body(0, 0, 0)
            with eng.Fori(0, NA // NBUF - 1) as g4:
                for r in range(NBUF):
                    body(g4 * NBUF + (r + 1), (r + 1) % NBUF, g4 + (r + 1) // NBUF)
            for g in range(NA - NBUF + 1, NA):
                body(g, g % NBUF, g // NBUF)

        def is_last(g, n=0):
            return isinstance(g, int) and g >= NA - n

        def sp_phase3(sp):
            sp.wait_ge(s["filled"], 16)
            for hf in range(2):
                sp.wait_ge(q_sent[hf], NG * 16)
                sp.wait_ge(k_sent[hf], NG * 16)

            def load(g, r, gb):
                for i, (qp, kp) in enumerate(zip(Q_PART, K_PART)):
                    for hf in range(2):
                        heads = slice(hf * HALF, (hf + 1) * HALF)
                        sp.dma_start(qst[r][i * EX:(i + 1) * EX, heads],
                                     qparts[hf, :, qp, bass.ds(g * JA * S, JA * S)].rearrange("(h e) t -> e h t", e=EX)).then_inc(q_in[r], 16)
                        sp.dma_start(kst[r][i * EX:(i + 1) * EX, heads],
                                     kparts[hf, :, kp, bass.ds(g * JA * KEYS, JA * KEYS)].rearrange("(h e) t -> e h t", e=EX)).then_inc(k_in[r], 16)

            def shift(g, r):
                sp.wait_ge(s["mT"], g + 1)
                for j in range(JA):
                    for i in range(PARTS):
                        at = (j * (PARTS + 1) + i) * HEADS
                        sp.dma_start(qst[r][ROWS + i:ROWS + i + 1, :, j * S:(j + 1) * S], mT[r % 2][at:at + HEADS]).then_inc(m_in[r], 16)

            load(0, 0, 0)
            load(1, 1, 0)
            load(2, 2, 0)

            def step_a(g, r, gb):
                shift(g, r)

            def body(g, r, gb):
                if not is_last(g, 3):
                    if not (is_first(g)):
                        sp.wait_ge(s["bp"], g * (4 * JA))
                    load(g + 3, (r + 3) % NBUF, None)
                if not is_last(g, 2):
                    shift(g + 2, (r + 2) % NBUF)
            loop3(sp, body, step_a)

        def pe_phase3(pe):
            def scores(g, r, j):
                for u, (h0, h1) in enumerate(UNITS):
                    n = j * 3 + u
                    if not (is_first(g) and n < 2):
                        pe.wait_ge(s["amax"], g * (3 * JA) + (n - 1))
                    for h in range(h0, h1):
                        i = pe.matmul(bank[n % 2][:, (h - h0) * KEYS:(h - h0 + 1) * KEYS],
                                      qst[r][0:ROWS, h, j * S:(j + 1) * S], kst[r][0:ROWS, h, j * KEYS:(j + 1) * KEYS],
                                      start=True, stop=True)
                    i.then_inc(s["ap"], 1)

            def turn_shift(g):
                if not is_first(g):
                    pe.wait_ge(s["mT"], g)
                pe.wait_ge(s["mlo"], g + 1)
                pe.transpose(bank[7][:, 256:256 + S // 2].bitcast(BF16), mpart[:].rearrange("p j a h -> p (j a h)"),
                             ident_b[:]).then_inc(s["mTp"], 1)

            def step_a(g, r, gb):
                pe.wait_ge(q_in[r], gb * (16 * 12) + 16 * 12)
                pe.wait_ge(k_in[r], gb * (16 * 12) + 16 * 12)
                for j in range(JA):
                    scores(g, r, j)
                turn_shift(g)

            def attend(g, r, j, tails, mid):
                for u in range(5):
                    if u < 4:
                        n = j * 4 + u
                        if not (is_first(g) and n < 2):
                            pe.wait_ge(s["expd"], g * (4 * JA) + (n - 1))
                        for c in range(4):
                            h = 4 * u + c
                            i = pe.matmul(bank[2 + u % 2][0:KEYS, c * S:(c + 1) * S],
                                          kst[r][0:SHIFT_ROWS, h, j * KEYS:(j + 1) * KEYS],
                                          qst[r][0:SHIFT_ROWS, h, j * S:(j + 1) * S], start=True, stop=True)
                        i.then_inc(s["bp"], 1)
                    if u == 0 and mid:
                        mid()
                    if u < len(tails):
                        tails[u]()
                    if u > 0:
                        n = j * 4 + u - 1
                        pe.wait_ge(s["expd"], g * (4 * JA) + (n + 1))
                        if u == 1:
                            pe.wait_ge(s["v_cur"], g * JA + (j + 1))
                        if u == 1 and not (is_first(g) and j == 0):
                            pe.wait_ge(s["avs"], g * JA + j)
                        for c in range(4):
                            i = pe.matmul(bank[4][32 * c:32 * c + EX + 1, (u - 1) * P:u * P],
                                          av_lhs(g, r, j, 4 * (u - 1) + c), prob[(u - 1) % 2][:, c],
                                          start=True, stop=True)
                        i.then_inc(s["avp"], 1)

            def av_lhs(g, r, j, h):
                return vcur[(r % 2) * JA + j][:, h]

            def tail(g, j):
                def t1():
                    pe.wait_ge(s["avs"], g * JA + (j + 1))
                    for u in range(4):
                        i = pe.transpose(bank[6][:, u * P:(u + 1) * P], avs[:, u * P:(u + 1) * P], ident[:])
                    i.then_inc(s["tavp"], 1)

                def t2():
                    pe.wait_ge(s["avn"], g * JA + (j + 1))
                    for k in range(2):
                        i = pe.transpose(bank[7][:, k * P:(k + 1) * P], avn[:, k * HALF:(k + 1) * HALF].rearrange("p h e -> p (h e)"), ident[:])
                    i.then_inc(s["t2p"], 1)

                def t3():
                    pe.wait_ge(s["t2"], g * JA + (j + 1))
                    for k in range(2):
                        i = pe.matmul(bank[5][:, 0:D], avnT[:, k * P:(k + 1) * P], fcw[:, k], start=(k == 0), stop=(k == 1))
                    i.then_inc(s["fcp"], 1)
                return [lambda: None, t1, t2, t3]

            def body(g, r, gb):
                pe.wait_ge(m_in[r], gb * (16 * PARTS * JA) + 16 * PARTS * JA)
                first = is_first(g)
                more = not is_last(g, 2)
                rn_, gn = (r + 2) % NBUF, (gb if r < 2 else gb + 1)

                def ahead(j):
                    def f():
                        if j == 0:
                            pe.wait_ge(q_in[rn_], gn * (16 * 12) + 16 * 12)
                            pe.wait_ge(k_in[rn_], gn * (16 * 12) + 16 * 12)
                        scores(g + 2, rn_, j)
                    return f
                attend(g, r, 0, [] if first else tail(g - 1, 1), ahead(0) if more else None)
                attend(g, r, 1, tail(g, 0), ahead(1) if more else None)
                if more:
                    turn_shift(g + 2)
            pe.wait_ge(s["ones_rows"], 2)
            loop3(pe, body, step_a)
            for f in tail(NA - 1, 1):
                f()


        def dve_phase3(v):
            def step_a(g, r, gb):
                for n in range(3 * JA):
                    maxima(g, n)
                parts(g)

            def maxima(g, n):
                h0, h1 = UNITS[n % 3]
                v.wait_ge(s["ap"], g * (3 * JA) + (n + 1))
                v.tensor_reduce(mx[:, n // 3, h0:h1], bank[n % 2][:, 0:(h1 - h0) * KEYS].rearrange("p (h k) -> p h k", k=KEYS),
                                AX.X, ALU.max).then_inc(s["amax"], 1)

            def parts(g):
                v.wait_ge(s["amax"], g * (3 * JA) + 3 * JA)
                v.tensor_scalar(mx[:], mx[:], -1.0, None, ALU.mult).then_inc(s["neg"], 1)
                v.wait_ge(s["neg"], g + 1)
                v.tensor_copy(mpart[:, :, 0], mx[:]).then_inc(s["mhi"], 1)
                v.wait_ge(s["mhi"], g + 1)
                v.tensor_tensor(mres[:], mx[:], mpart[:, :, 0], ALU.subtract).then_inc(s["mres"], 1)
                v.wait_ge(s["mres"], g + 1)
                v.tensor_copy(mpart[:, :, 1], mres[:]).then_inc(s["mmid"], 1)
                v.wait_ge(s["mmid"], g + 1)
                v.tensor_tensor(mpart[:, :, 2], mres[:], mpart[:, :, 1], ALU.subtract).then_inc(s["mlo"], 1)

            def tail(g, j, stage):
                b = g * JA + j
                if stage == 1:
                    v.wait_ge(s["tavp"], b + 1)
                    av = bank[6][:].rearrange("p (h w) -> p h w", w=32)
                    v.reciprocal(rden[:], av[:, :, EX:EX + 1].rearrange("p h o -> p (h o)")).then_inc(s["rden"], 1)
                    v.wait_ge(s["rden"], b + 1)
                    v.tensor_tensor(avn[:], av[:, :, 0:EX], rden[:].rearrange("p (h o) -> p h o", o=1).broadcast_to([P, HEADS, EX]),
                                    ALU.mult).then_inc(s["avn"], 1)
                if stage == 2:
                    v.wait_ge(s["fcp"], b + 1)
                    x_b = xs[:, bass.ds(b, 1)].rearrange("p o f -> p (o f)")
                    v.tensor_tensor(x_b, bank[5][:, 0:D], x_b, ALU.add).then_inc(s["x2"], 1)
                    wait_on_copy(v, s["x2"], b + 1)
                    v.bn_stats(stats3[:, bass.ds(b, 1)].rearrange("p o f -> p (o f)"), x_b).then_inc(s["stat3"], 1)

            def body(g, r, gb):
                first = is_first(g)
                more = not is_last(g, 2)
                for j in range(JA):
                    back = None if (first and j == 0) else ((g - 1, 1) if j == 0 else (g, 0))
                    if more:
                        maxima(g + 2, j * 3)
                        maxima(g + 2, j * 3 + 1)
                    if back:
                        tail(*back, 1)
                    if more:
                        maxima(g + 2, j * 3 + 2)
                    if back:
                        tail(*back, 2)
                    v.wait_ge(s["avp"], g * (4 * JA) + (4 * j + 4))
                    v.tensor_copy(avs[:], bank[4][:]).then_inc(s["avs"], 1)
                if more:
                    parts(g + 2)
            v.wait_ge(s["filled"], 16)
            v.memset(mpart[:], 0.0)
            for k in range(2):
                v.memset(kst[2 * k][ROWS:SHIFT_ROWS], 1.0)
                v.memset(kst[2 * k + 1][ROWS:SHIFT_ROWS], 1.0).then_inc(s["ones_rows"], 1)
            v.wait_ge(s["xb2"], 1)
            loop3(v, body, step_a)
            tail(NA - 1, 1, 1)
            tail(NA - 1, 1, 2)

        def act_phase3(a):
            def copy_shift(g, r):
                a.wait_ge(s["mTp"], g + 1)
                a.copy(mT[r % 2][:], bank[7][:, 256:256 + S // 2].bitcast(BF16)).then_inc(s["mT"], 1)

            def step_a(g, r, gb):
                copy_shift(g, r)

            def body(g, r, gb):
                first = is_first(g)
                for j in range(JA):
                    back = None if (first and j == 0) else (g * JA + j - 1)
                    for u in range(4):
                        n = j * 4 + u
                        a.wait_ge(s["bp"], g * (4 * JA) + (n + 1))
                        if not (first and n < 2):
                            a.wait_ge(s["avp"], g * (4 * JA) + (n - 1))
                        a.activation(prob[u % 2][:].rearrange("p c t -> p (c t)"), bank[2 + u % 2][0:KEYS], ACT.Exp,
                                     scale=SCORE_SCALE).then_inc(s["expd"], 1)
                        if u == 2 and back is not None:
                            a.wait_ge(s["t2p"], back + 1)
                            a.copy(avnT[:], bank[7][:, 0:2 * P]).then_inc(s["t2"], 1)
                if not is_last(g, 2):
                    copy_shift(g + 2, (r + 2) % NBUF)
            loop3(a, body, step_a)
            a.wait_ge(s["t2p"], B)
            a.copy(avnT[:], bank[7][:, 0:2 * P]).then_inc(s["t2"], 1)


        def pool_phase3(p):
            p.wait_ge(s["xn2"], NG)
            p.tensor_tensor(xs[:], xs[:], fcb[:].rearrange("p (o f) -> p o f", o=1).broadcast_to([P, B, D]),
                            ALU.add).then_inc(s["xb2"], 1)
            p.wait_ge(s["v_ready"], 2 * NG)
            p.wait_ge(s["filled"], 16)

            def copy_values(b, k):
                p.tensor_copy(vcur[k][:], vals[:, bass.ds(b, 1)].rearrange("p o h e -> p (o h) e")).then_inc(s["v_cur"], 1)
            for b in range(2 * JA):
                copy_values(b, b)
            with p.Fori(1, B // (2 * JA)) as i:
                for k in range(2 * JA):
                    p.wait_ge(s["avp"], i * (4 * 2 * JA) + (4 * (k + 1) - 4 * 2 * JA))
                    copy_values(i * (2 * JA) + k, k)

        sb4 = late()
        N_LG = B * EXPERTS
        h_rows = sb4("h_rows", [P, B, ROW])
        lgT = sb4("lgT_s", [EXPERTS, GT])
        lg = sb4("lg_s", [P, N_LG])
        best = sb4("best", [P, B])
        wrk = sb4("wrk", [P, N_LG])
        low = sb4("low", [P, B])
        oh = sb4("oh_s", [P, N_LG])
        oh_b = sb4("oh_b", [P, N_LG], BF16)
        tot = sb4("tot", [P, N_LG])
        cum = sb4("cum", [P, N_LG])
        onesf = sb4("onesf", [P, N_LG])
        cnt = sb4("cnt", [P, EXPERTS])
        cnt_i = sb4("cnt_i", [P, EXPERTS], I32)
        tiles_f = sb4("tiles_f", [P, EXPERTS])
        tile_end = sb4("tile_end", [P, EXPERTS])
        adj = sb4("adj", [P, EXPERTS])
        esc = sb4("esc_s", [P, B])
        score = sb4("score_s", [P, B])
        posf = sb4("posf", [P, B])
        pos = sb4("pos_s", [P, B], I32)
        owner_w = sb4("owner_w", [P, TILES, EXPERTS])
        owner_f = sb4("owner_f", [P, TILES])
        owner = sb4("owner", [P, TILES], I32)
        s_g = [sb4(f"s_g{i}", [P, GT]) for i in range(2)]
        act = [sb4(f"act{i}", [P, GT]) for i in range(CH)]
        t_row = [sb4(f"t_row{i}", [P, ROW]) for i in range(NBUF)]
        t_gu = [sb4(f"t_gu{i}", [P, FF2]) for i in range(NBUF)]
        t_dn = [sb4(f"t_dn{i}", [P, D]) for i in range(NBUF)]
        t_hT = [sb4(f"t_hT{i}", [P, P]) for i in range(2)]
        t_sg = [sb4(f"t_sg{i}", [P, P]) for i in range(2)]
        t_act = [sb4(f"t_act{i}", [P, P]) for i in range(2)]
        t_y = [sb4(f"t_y{i}", [P, D]) for i in range(NBUF)]
        y_back = [sb4(f"y_back{i}", [P, JP, D]) for i in range(2)]

        def bc(ap, n):
            return ap.rearrange("p (m o) -> p m o", o=1).broadcast_to([P, ap.shape[1], n])

        def rep(ap, n):
            return ap.rearrange("p (o m) -> p o m", o=1).broadcast_to([P, n, ap.shape[1]])

        def dve_phase4(v):
            def step(i):
                steps[0] += 1
                i.then_inc(s["r_step"], 1)
                v.wait_ge(s["r_step"], steps[0])
            steps = [0]
            v.wait_ge(s["stat3"], B)
            for b in range(B):
                i = v.bn_aggr(mv[:, b], stats3[:, b])
            i.then_inc(s["mean3"], 1)
            v.wait_ge(s["std3"], 1)
            step(v.reciprocal(rstd[:], std[:]))
            for g in range(NG):
                if g >= 2:
                    v.wait_ge(s["hTp"], g - 1)
                    v.wait_ge(s["h_kept"], g - 1)
                for j in range(JP):
                    b = g * JP + j
                    i = v.tensor_scalar(xn[g % 2][:, j], xs[:, b], mv[:, b, 0:1], rstd[:, b:b + 1], ALU.subtract, ALU.mult)
                i.then_inc(s["xn3"], 1)
            v.wait_ge(s["lgtp"], NG)
            step(v.tensor_copy(lg[:], bank[3][:]))
            lg3 = lg[:].rearrange("p (b n) -> p b n", n=EXPERTS)
            wrk3 = wrk[:].rearrange("p (b n) -> p b n", n=EXPERTS)
            oh3 = oh[:].rearrange("p (b n) -> p b n", n=EXPERTS)
            v.memset(onesf[:], 1.0)
            step(v.tensor_reduce(best[:], lg3, AX.X, ALU.max))
            v.tensor_copy(esc[:], best[:]).then_inc(s["lg"], 1)
            step(v.tensor_tensor(wrk3, lg3, bc(best[:], EXPERTS), ALU.is_equal))
            step(v.scalar_tensor_tensor(out=wrk3, in0=wrk3, scalar=-float(EXPERTS), in1=rep(expert_no[:], B),
                                        op0=ALU.mult, op1=ALU.add))
            step(v.tensor_reduce(low[:], wrk3, AX.X, ALU.min))
            step(v.tensor_tensor(oh3, wrk3, bc(low[:], EXPERTS), ALU.is_equal))
            v.tensor_copy(oh_b[:], oh[:]).then_inc(s["oh"], 1)
            v.wait_ge(s["escore"], 1)
            step(v.tensor_scalar(esc[:], score[:], 1.0, None, ALU.add))
            v.reciprocal(posf[:], esc[:]).then_inc(s["sc_ready"], 1)
            v.wait_ge(s["rankp"], 1)
            tot3 = tot[:].rearrange("p (n b) -> p n b", b=B)
            cum3 = cum[:].rearrange("p (n b) -> p n b", b=B)
            step(v.tensor_copy(tot3, bank[6][:].rearrange("p (b n) -> p n b", n=EXPERTS)))
            step(v.tensor_tensor_scan(out=cum[:], data0=onesf[:], data1=tot[:], initial=0.0, op0=ALU.mult, op1=ALU.add))
            step(v.tensor_tensor(tot[:], cum[:], tot[:], ALU.subtract))
            first, last = tot3[:, :, 0], cum3[:, :, B - 1]
            step(v.tensor_tensor(cnt[:], last, first, ALU.subtract))
            step(v.tensor_scalar(cnt[:], cnt[:], float(P - 1), None, ALU.add))
            step(v.tensor_copy(cnt_i[:], cnt[:]))
            step(v.tensor_scalar(cnt_i[:], cnt_i[:], 7, None, ALU.logical_shift_right))
            step(v.tensor_copy(tiles_f[:], cnt_i[:]))
            step(v.tensor_tensor_scan(out=tile_end[:], data0=onesf[:, 0:EXPERTS], data1=tiles_f[:], initial=0.0,
                                      op0=ALU.mult, op1=ALU.add))
            step(v.tensor_tensor(adj[:], tile_end[:], tiles_f[:], ALU.subtract))
            step(v.scalar_tensor_tensor(out=adj[:], in0=adj[:], scalar=float(P), in1=first, op0=ALU.mult, op1=ALU.subtract))
            step(v.tensor_tensor(tot3, tot3, bc(adj[:], B), ALU.add))
            step(v.tensor_tensor(wrk3, bank[5][:].rearrange("p (b n) -> p b n", n=EXPERTS),
                                 tot[:].rearrange("p (n b) -> p b n", b=B), ALU.add))
            step(v.tensor_tensor(wrk[:], wrk[:], oh[:], ALU.mult))
            step(v.tensor_reduce(low[:], wrk3, AX.X, ALU.add))
            v.tensor_copy(pos[:], low[:]).then_inc(s["pos"], 1)
            step(v.tensor_tensor(owner_w[:], rep(tile_end[:], TILES), bc(tile_no[:], EXPERTS), ALU.is_le))
            step(v.tensor_reduce(owner_f[:], owner_w[:], AX.X, ALU.add))
            step(v.tensor_scalar(owner_f[:], owner_f[:], float(EXPERTS - 1), None, ALU.min))
            v.tensor_copy(owner[:], owner_f[:]).then_inc(s["etile"], 1)

            def shared(g, par):
                for c in range(CH):
                    v.wait_ge(s["silu"], g * CH + (c + 1))
                    v.tensor_tensor(act[c][:], bank[BK_UP[c % 2]][:], s_g[c % 2][:], ALU.mult).then_inc(s["act"], 1)
                    if c == 1 and not (is_first(g)):
                        add_down(g - 1, 1 - par)

            def add_down(g, par):
                v.wait_ge(s["downp"], g + 1)
                x_g = seqs(xs, g).rearrange("p j f -> p (j f)")
                v.tensor_tensor(x_g, bank[BK_DOWN[par]][:], x_g, ALU.add).then_inc(s["x3"], 1)
            loop_shared(v, shared)
            add_down(NG - 1, 1)

            def mul(n, r):
                v.wait_ge(s["tsilu"], n + 1)
                v.tensor_tensor(t_act[r % 2][:], bank[2 + r % 2][:, P:2 * P], t_sg[r % 2][:], ALU.mult).then_inc(s["tact"], 1)

            def leave(n, r, k):
                v.wait_ge(s["tyd"], n + 1)
                if not (isinstance(n, int) and n < NBUF):
                    v.wait_ge(t_out[r], k * 16)
                v.tensor_copy(t_y[r][:], bank[4 + r % 2][:, 0:D]).then_inc(s["ty"], 1)

            def body(n, r, k):
                if not last_tile(n, 1):
                    mul(n + 1, (r + 1) % NBUF)
                leave(n, r, k)
            mul(0, 0)
            loop_tiles(v, body)

            for g in range(NG):
                v.wait_ge(y_in[g % 2], (g // 2 + 1) * 16)
                v.tensor_tensor(xs[:, g * JP:(g + 1) * JP], xs[:, g * JP:(g + 1) * JP], y_back[g % 2][:], ALU.add).then_inc(s["res_add"], 1)

        BK_GATE, BK_UP, BK_DOWN = (0, 1), (2, 7), (3, 4)

        def loop_shared(eng, body):
            body(0, 0)
            with eng.Fori(0, NG // 2 - 1) as g2:
                for k in range(2):
                    body(g2 * 2 + (k + 1), (k + 1) % 2)
            body(NG - 1, 1)

        def last_tile(n, lead):
            return isinstance(n, int) and n >= TILES - lead

        def loop_tiles(eng, body):
            for n in range(NBUF):
                body(n, n, 0)
            with eng.Fori(1, TILES // NBUF - 1) as k:
                for r in range(NBUF):
                    body(k * NBUF + r, r, k)
            for n in range(TILES - NBUF, TILES):
                body(n, n % NBUF, n // NBUF)

        def act_phase4(a):
            a.wait_ge(s["mean3"], 1)
            a.activation(std[:], mv[:, :, 1], ACT.Sqrt, bias=eps[:]).then_inc(s["std3"], 1)
            for g in range(NG):
                a.wait_ge(s["hTp"], g + 1)
                a.copy(xT[:, g * GT:(g + 1) * GT], bank[0 + g % 2][:]).then_inc(s["hT"], 1)
                a.wait_ge(s["lgp"], g + 1)
                a.copy(lgT[:], bank[2][0:EXPERTS]).then_inc(s["lgT"], 1)
            a.wait_ge(s["lg"], 1)
            a.activation(score[:], esc[:], ACT.Exp, scale=-1.0).then_inc(s["escore"], 1)

            def shared(g, par):
                for c in range(CH):
                    a.wait_ge(s["gup"], g * CH + (c + 1))
                    if not (is_first(g) and c < 2):
                        a.wait_ge(s["act"], g * CH + (c - 1))
                    a.activation(s_g[c % 2][:], bank[BK_GATE[c % 2]][:], ACT.Silu).then_inc(s["silu"], 1)
            a.wait_ge(s["sc_ready"], 1)
            a.wait_ge(s["h_kept"], NG)
            for b in range(B):
                a.activation(h_rows[:, b, 0:D], h_rows[:, b, 0:D], ACT.Copy, scale=posf[:, b:b + 1]).then_inc(s["rows"], 1)
            loop_shared(a, shared)

            def turned(n, r):
                a.wait_ge(s["tTp"], n + 1)
                a.copy(t_hT[r % 2][:], bank[0 + r % 2][:, 0:P]).then_inc(s["tT"], 1)

            def gated(n, r):
                a.wait_ge(s["tgup"], n + 1)
                a.activation(t_sg[r % 2][:], bank[2 + r % 2][:, 0:P], ACT.Silu).then_inc(s["tsilu"], 1)

            def body(n, r, k):
                if not last_tile(n, 2):
                    turned(n + 2, (r + 2) % NBUF)
                if not last_tile(n, 1):
                    gated(n + 1, (r + 1) % NBUF)
            turned(0, 0)
            turned(1, 1)
            gated(0, 0)
            loop_tiles(a, body)

        def pool_phase4(p):
            p.wait_ge(s["x2"], B)
            p.memset(h_rows[:, :, D:ROW], 0.0).then_inc(s["rows"], 1)
            p.wait_ge(s["rows"], 1)
            p.tensor_copy(h_rows[:, :, D:D + 1].bitcast(I32).rearrange("p b o -> p (b o)"), token_no[:])
            for g in range(NG):
                p.wait_ge(s["xn3"], g + 1)
                p.tensor_copy(h_rows[:, g * JP:(g + 1) * JP, 0:D], xn[g % 2][:]).then_inc(s["h_kept"], 1)
            p.wait_ge(s["pos"], 1)
            p.wait_ge(s["rows"], 1 + B)
            p.wait_ge(s["filled"], 16)
            for b in range(B):
                p.indirect_dma_start(out=sorted_in, out_offset=bass.IndirectOffsetOnAxis(ap=pos[:, b:b + 1].bitcast(U32), axis=0),
                                     in_=h_rows[:, b], in_offset=None).then_inc(s["scat"], 16)

            def body(n, r, k):
                if not is_first(n):
                    p.wait_ge(s["carried"], n)
                p.wait_ge(s["ty"], n + 1)
                p.tensor_tensor(carrier_p[:], eps_p[:], eps_p[:], ALU.add).then_inc(s["carried"], 1)
                p.indirect_dma_start(out=routed, out_offset=bass.IndirectOffsetOnAxis(ap=t_row[r][:, D:D + 1].bitcast(U32), axis=0),
                                     in_=t_y[r][:], in_offset=None).then_inc(t_out[r], 16)
            loop_tiles(p, body)

        def pe_phase4(pe):
            for g in range(NG):
                pe.wait_ge(s["xn3"], g + 1)
                for j in range(JP):
                    i = pe.transpose(bank[0 + g % 2][:, j * P:(j + 1) * P], xn[g % 2][:, j], ident[:])
                i.then_inc(s["hTp"], 1)
                pe.wait_ge(s["hT"], g + 1)
                pe.matmul(bank[2][0:EXPERTS], rw[:], xT[:, g * GT:(g + 1) * GT], start=True, stop=True).then_inc(s["lgp"], 1)
                pe.wait_ge(s["lgT"], g + 1)
                for j in range(JP):
                    b = g * JP + j
                    i = pe.transpose(bank[3][:, b * EXPERTS:(b + 1) * EXPERTS], lgT[:, j * P:(j + 1) * P], ident[0:EXPERTS, 0:EXPERTS])
                i.then_inc(s["lgtp"], 1)
            pe.wait_ge(s["oh"], 1)
            pe.matmul(bank[5][:], before[:], oh_b[:], start=True, stop=True)
            pe.matmul(bank[6][:], ones_b[:], oh_b[:], start=True, stop=True).then_inc(s["rankp"], 1)

            def down(g, par, c):
                pe.wait_ge(s["act"], g * CH + (c + 1))
                for j in range(JP):
                    i = pe.matmul(bank[BK_DOWN[par]][:, j * D:(j + 1) * D], act[c][:, j * P:(j + 1) * P], sd[:, c],
                                  start=(c == 0 and j == 0), stop=(c == CH - 1), skip_group_check=True)
                if c == CH - 1:
                    i.then_inc(s["downp"], 1)

            def shared(g, par):
                first = is_first(g)
                for c in range(CH):
                    if not (first and c < 2):
                        pe.wait_ge(s["act"], g * CH + (c - 1))
                    pe.matmul(bank[BK_GATE[c % 2]][:], sg[:, c * P:(c + 1) * P], xT[:, bass.ds(g * GT, GT)], start=True, stop=True)
                    pe.matmul(bank[BK_UP[c % 2]][:], su[:, c * P:(c + 1) * P], xT[:, bass.ds(g * GT, GT)],
                              start=True, stop=True).then_inc(s["gup"], 1)
                    if c > 0:
                        down(g, par, c - 1)
                    elif not first:
                        down(g - 1, 1 - par, CH - 1)
            pe.wait_ge(s["r_step"], 2)
            loop_shared(pe, shared)
            down(NG - 1, 1, CH - 1)

            def turn(n, r, k):
                pe.wait_ge(t_in[r], k * 48 + 48)
                i = pe.transpose(bank[0 + r % 2][:, 0:P], t_row[r][:, 0:D], ident[:])
                i.then_inc(s["tTp"], 1)

            def gate_up(n, r):
                pe.wait_ge(s["tT"], n + 1)
                if not (isinstance(n, int) and n < 2):
                    pe.wait_ge(s["tact"], n - 1)
                pe.matmul(bank[2 + r % 2][:, 0:P], t_gu[r][:, 0:FF], t_hT[r % 2][:], start=True, stop=True)
                pe.matmul(bank[2 + r % 2][:, P:2 * P], t_gu[r][:, FF:FF2], t_hT[r % 2][:], start=True, stop=True).then_inc(s["tgup"], 1)

            def body(n, r, k):
                if not last_tile(n, 2):
                    turn(n + 2, (r + 2) % NBUF, k + (r + 2) // NBUF)
                if not last_tile(n, 1):
                    gate_up(n + 1, (r + 1) % NBUF)
                pe.wait_ge(s["tact"], n + 1)
                if not (isinstance(n, int) and n < 2):
                    pe.wait_ge(s["ty"], n - 1)
                pe.matmul(bank[4 + r % 2][:, 0:D], t_act[r % 2][:], t_dn[r][:], start=True, stop=True).then_inc(s["tyd"], 1)
            pe.wait_ge(s["x3"], NG)
            turn(0, 0, 0)
            turn(1, 1, 0)
            gate_up(0, 0)
            loop_tiles(pe, body)

        def sp_phase4(sp):
            def load(n, r, k):
                e = sp.value_load(owner[0:1, bass.ds(n, 1)], min_val=0, max_val=EXPERTS - 1)
                again = not (isinstance(n, int) and n < NBUF)
                if again:
                    sp.wait_ge(s["tyd"], n - (NBUF - 1))
                sp.dma_start(t_gu[r][:], t["L0_ffn_gate_up_proj"][bass.ds(e, 1)].rearrange("o h f -> (o h) f")).then_inc(t_in[r], 16)
                sp.dma_start(t_dn[r][:], t["L0_ffn_down_proj"][bass.ds(e, 1)].rearrange("o h f -> (o h) f")).then_inc(t_in[r], 16)
                if again:
                    sp.wait_ge(t_out[r], k * 16)
                sp.dma_start(t_row[r][:], sorted_in[bass.ds(n * P, P)]).then_inc(t_in[r], 16)
            sp.wait_ge(s["etile"], 1)
            sp.wait_ge(s["scat"], B * 16)
            loop_tiles(sp, load)
            for r in range(NBUF):
                sp.wait_ge(t_out[r], TILES // NBUF * 16)
            for g in range(NG):
                if g >= 2:
                    sp.wait_ge(s["res_add"], g - 1)
                sp.dma_start(y_back[g % 2][:], routed[g * GT:(g + 1) * GT].rearrange("(j p) f -> p j f", p=P)).then_inc(y_in[g % 2], 16)
                if g >= 1:
                    store(sp, g - 1)
            store(sp, NG - 1)
            sp.wait_ge(s["res_out"], NG * 16)

        def store(sp, g):
            sp.wait_ge(s["res_add"], g + 1)
            sp.dma_start(out[g * JP:(g + 1) * JP].rearrange("b p f -> p b f"), xs[:, g * JP:(g + 1) * JP]).then_inc(s["res_out"], 16)

        fill = late()("fill", [P, TILES, ROW])

        def sp_fill(sp):
            sp.wait_ge(s["fill_set"], 2)
            sp.dma_start(sorted_in.rearrange("(p j) r -> p j r", p=P), fill[:]).then_inc(s["filled"], 16)
            for dst, name in LATE:
                sp.dma_start(ap_of(dst), t[name]).then_inc(s["weights_in"], 16)

        def pool_fill(p):
            p.memset(eps_p[:], 0.0)
            p.memset(fill[:], 0.0).then_inc(s["fill_set"], 1)
            p.wait_ge(s["const_in"], N_CONST)
            p.wait_ge(s["fill_set"], 1)
            p.tensor_copy(fill[:, :, D:D + 1].bitcast(I32).rearrange("p j o -> p (j o)"), slot_no[:]).then_inc(s["fill_set"], 1)

        block = ctx.enter_context(nc.Block())

        @block.sync
        def _(sp):
            sp_phase0(sp)
            sp_phase1(sp)
            sp_fill(sp)
            sp_phase2(sp)
            sp_phase3(sp)
            sp_phase4(sp)

        @block.gpsimd
        def _(p):
            pool_fill(p)
            pool_phase1(p)
            pool_phase3(p)
            pool_phase4(p)

        @block.tensor
        def _(pe):
            pe_phase1(pe)
            pe_phase2(pe)
            pe_phase3(pe)
            pe_phase4(pe)

        @block.vector
        def _(v):
            dve_phase0(v)
            dve_phase1(v)
            dve_phase2(v)
            dve_phase3(v)
            dve_phase4(v)

        @block.scalar
        def _(a):
            act_phase0(a)
            act_phase1(a)
            act_phase2(a)
            act_phase3(a)
            act_phase4(a)


def kernel(**inputs):
    import numpy as np
    import concourse.bacc as bacc
    from concourse.bass_utils import run_bass_kernel_spmd

    x = np.ascontiguousarray(inputs["x"])
    B, S, D = x.shape
    experts = inputs["L0_ffn_router_w"].shape[0]
    tiles = B * S // P + experts
    sf = inputs["L0_ffn_shared_gate_w"].shape[0]
    arrays = {"x": x}
    for name in ("ctx_1024", "L0_attn_Wq", "L0_attn_Wk", "L0_attn_Wv", "L0_attn_Wo", "L0_attn_bq", "L0_attn_bk",
                 "L0_attn_bv", "L0_attn_bo", "L0_xattn_fc_b", "L0_ffn_gate_up_proj", "L0_ffn_down_proj"):
        arrays[name] = inputs[name]
    fm_w = np.asarray(inputs["L0_xattn_fm_w"])
    arrays["fm_wT"] = np.tile(fm_w.T, (HEADS, 2 * HALF * 2)).reshape(P, 2, P)
    arrays["fm_b"] = np.tile(np.asarray(inputs["L0_xattn_fm_b"]), HEADS).reshape(P, 1)
    arrays["m_col"] = np.repeat(np.asarray(inputs["L0_attn_m"]), HD).reshape(P, 1)
    arrays["fc_wT"] = np.asarray(inputs["L0_xattn_fc_w"]).T.reshape(2, P, D).transpose(1, 0, 2)
    arrays["router_wT"] = np.asarray(inputs["L0_ffn_router_w"]).T
    arrays["shared_gateT"] = np.asarray(inputs["L0_ffn_shared_gate_w"]).T
    arrays["shared_upT"] = np.asarray(inputs["L0_ffn_shared_up_w"]).T
    arrays["shared_downT"] = np.asarray(inputs["L0_ffn_shared_down_w"]).T.reshape(sf // P, P, D).transpose(1, 0, 2)
    r = np.arange(P)
    f32 = np.float32
    arrays["ident"] = np.eye(P, dtype=f32)
    arrays["headmask"] = (r[:, None] // HD == r[None, :] // HD).astype(f32)
    sign = np.where(r % EX < HD, 1, -1)
    arrays["signs"] = np.stack([np.where(r[:, None] // HD == hf * HALF + r[None, :] // EX, sign[None, :], 0)
                                for hf in range(2)], axis=1).astype(f32)
    arrays["signcol"] = sign.astype(f32).reshape(P, 1)
    arrays["before"] = (r[:, None] < r[None, :]).astype(f32)
    arrays["expert_no"] = np.tile(np.arange(experts, dtype=f32), (P, 1))
    arrays["tile_no"] = np.tile(np.arange(tiles, dtype=f32), (P, 1))
    arrays["token_no"] = (np.arange(B)[None, :] * P + r[:, None]).astype(np.int32)
    arrays["slot_no"] = (B * S + np.arange(P * tiles).reshape(P, tiles)).astype(np.int32)

    nc = bacc.Bacc("TRN2", target_bir_lowering=False, num_devices=1)
    feed, t = {}, {}
    for name, a in arrays.items():
        a = np.ascontiguousarray(a)
        feed[f"in_{name}"] = a
        t[name] = nc.dram_tensor(f"in_{name}", a.shape, mybir.dt.from_np(a.dtype), kind="ExternalInput").ap()
    out = nc.dram_tensor("out_x", (B, S, D), F32, kind="ExternalOutput").ap()
    decoder_layer(nc, t, out)
    r = run_bass_kernel_spmd(nc, [feed], core_ids=[0])
    return r.results[0]["out_x"]
```

```python
import math
from contextlib import ExitStack

import concourse.bass as bass
from concourse import mybir

ALU = mybir.AluOpType
ACT = mybir.ActivationFunctionType
AX = mybir.AxisListType
F32 = mybir.dt.float32
BF16 = mybir.dt.bfloat16
I32 = mybir.dt.int32
U32 = mybir.dt.uint32

P = 128
HEADS, HD = 16, 8
EX = 2 * HD
HALF = HEADS // 2
LN_EPS, L2_EPS = 1e-5, 1e-12
PARTS = 3
Q_PART = (0, 0, 0, 1, 1, 2)
K_PART = (0, 1, 2, 0, 1, 0)
Q_RUNS = ((0, 0, 3), (3, 1, 2), (5, 2, 1))
K_RUNS = ((0, 0, 3), (3, 0, 2), (5, 0, 1))
ROWS = len(Q_PART) * EX
SHIFT_ROWS = ROWS + PARTS


def decoder_layer(nc, t, out):
    B, S, D = t["x"].shape
    KEYS = t["ctx_1024"].shape[1]
    EXPERTS, _, FF3 = t["expert_w"].shape
    FF = FF3 // 3
    SF = t["shared_gateT"].shape[1]
    CH = SF // P
    TOK = B * S
    JP = 4
    NG = B // JP
    GT = JP * S
    JK = JP * KEYS
    JA = 2
    NA = B // JA
    NBUF = 4
    RING = 8
    TILES = TOK // P + EXPERTS
    SLOTS = TILES * P
    ROW = D + 4
    assert S == D == P and FF == P and HEADS * HD == D and GT == 512
    SCORE_SCALE = float(D) ** -0.5
    UNITS = ((0, 6), (6, 11), (11, 16))

    with ExitStack() as ctx:
        def sb(name, shape, dt=F32):
            return ctx.enter_context(nc.sbuf_tensor(name, shape, dt))

        def arena(name, size):
            start = nc.sbuf_base
            ctx.enter_context(nc.sbuf_tensor(name, [P, size // 4], F32))

            def phase():
                at = [start]

                def place(n, shape, dt=F32):
                    tile = nc.alloc_sbuf_tensor_at(n, shape, dt, offset=at[0])
                    words = 1
                    for d in shape[1:]:
                        words *= d
                    at[0] += -(-words * mybir.dt.size(dt) // 32) * 32
                    assert at[0] <= start + size, (n, at[0] - start)
                    return tile
                return place
            return phase

        def sem(name):
            return ctx.enter_context(nc.semaphore(name))

        bank = [ctx.enter_context(nc.psum_tensor(f"bank{i}", [P, 512], F32)) for i in range(8)]

        qparts = nc.dram_tensor("qparts", (HEADS, EX, PARTS, TOK), BF16).ap()
        kparts = nc.dram_tensor("kparts", (PARTS, EX, HEADS, B * KEYS), BF16).ap()
        sorted_in = nc.dram_tensor("sorted_in", (SLOTS, ROW), F32).ap()
        routed = nc.dram_tensor("routed", (TOK + SLOTS, D), F32).ap()

        ident = sb("ident_s", [P, P])
        ident_b = sb("ident_b", [P, P], BF16)
        headmask = sb("headmask_s", [P, P])
        signs = sb("signs_s", [P, 2, P])
        signcol = sb("signcol_s", [P, 1])
        before_f = sb("before_f", [P, P])
        before = sb("before_b", [P, P], BF16)
        ones_b = sb("ones_b", [P, P], BF16)
        expert_no = sb("expert_no", [P, EXPERTS])
        tile_no = sb("tile_no", [P, TILES])
        token_no = sb("token_no", [P, B], I32)
        slot_no = sb("slot_no_s", [P, TILES], I32)
        wqkv = sb("wqkv", [P, 3 * D])
        bqkv = sb("bqkv", [P, 3 * D])
        wo = sb("wo", [P, D])
        bo = sb("bo", [P, D])
        m_col = sb("m_col", [P, 1])
        inv_scale = sb("inv_scale", [P, 4])
        map_w = sb("map_w", [P, 2, P])
        map_b = sb("map_b", [P, 2])
        fcw = sb("fcw", [P, 2, D])
        fcb = sb("fcb", [P, D])
        rw = sb("rw", [P, EXPERTS])
        sg = sb("sg", [P, SF])
        su = sb("su", [P, SF])
        sd = sb("sd", [P, CH, D])
        eps = sb("eps", [P, 1])
        eps_p = sb("eps_p", [P, 1])
        carrier_p = sb("carrier_p", [P, 1])
        carrier = sb("carrier", [P, 1])

        xs = sb("xs", [P, B, D])
        xT = sb("xT", [P, TOK])
        vals = sb("vals", [KEYS, B, HEADS, EX + 1])
        stats3 = sb("stats3", [P, B, 6])
        mv = sb("mv", [P, B, 2])
        std = sb("std", [P, B])
        rstd = sb("rstd", [P, B])
        xn = [sb(f"xn{i}", [P, JP, D]) for i in range(2)]

        s = {}
        for n in ("const_in", "weights_in", "fill_set", "carried", "filled", "cast", "map_ready", "esc", "esc_dve",
                  "inv_ready", "stat1", "mean1", "std1", "rstd1", "bias1", "xn1", "xT1p", "xT1", "qkvp", "qkv1",
                  "sq1", "ss1", "nrm1", "nmax1", "rn1", "qkn1", "qTp", "qT1", "kvp", "mt1", "mwp", "mw1", "yp",
                  "xb1", "x1", "stat2", "mean2", "std2", "rstd2", "bias2", "xn2", "xT2p", "xT2", "zqp", "qf", "qhi",
                  "qres", "qmid", "qlo", "ctxTp", "ctxT", "zkp", "kf", "khi", "kres", "kmid", "klo", "vp", "v_ready",
                  "ap", "amax", "neg", "mhi", "mres", "mmid", "mlo", "mTp", "mT", "bp", "expd", "avp", "avs",
                  "ones_rows", "set", "v_cur", "tavp", "rden", "avn", "t2p", "t2", "fcp", "x2", "stat3", "mean3",
                  "xb2", "std3", "xn3", "h_kept", "hTp", "hT", "lgp", "lgT", "lgtp", "lg", "r_step", "oh", "rankp",
                  "escore", "sc_ready", "pos", "rows", "scat", "etile", "gup", "silu", "act", "downp", "x3", "tTp",
                  "tT", "tgup", "tsilu", "tact", "tyd", "ty", "res_add", "res_out"):
            s[n] = sem(n)
        x_in = [sem(f"x_in{i}") for i in range(2)]
        c_in = [sem(f"c_in{i}") for i in range(2)]
        parts_in = [sem(f"parts_in{i}") for i in range(NBUF)]
        m_in = [sem(f"m_in{i}") for i in range(NBUF)]
        q_sent = [[sem(f"q_sent{par}_{hf}") for hf in range(2)] for par in range(2)]
        k_sent = [[sem(f"k_sent{par}_{hf}") for hf in range(2)] for par in range(2)]
        t_in = [sem(f"t_in{i}") for i in range(RING)]
        t_out = [sem(f"t_out{i}") for i in range(RING)]
        y_in = [sem(f"y_in{i}") for i in range(2)]

        def seqs(tile, g, n=JP):
            return tile[:, bass.ds(g * n, n)]

        def is_first(g):
            return isinstance(g, int) and g == 0

        def wait_on_copy(v, semaphore, value):
            v.wait_ge(semaphore, value)
            v.tensor_copy(carrier[:], eps[:])

        CONSTS = [(ident, "ident"), (headmask, "headmask"), (signs, "signs"), (signcol, "signcol"),
                  (before_f, "before"), (expert_no, "expert_no"), (tile_no, "tile_no"), (token_no, "token_no"), (slot_no, "slot_no"),
                  (map_w, "fm_wT"), (map_b[:, 0:1], "fm_b"), (m_col, "m_col"),
                  (wqkv[:, 0:D], "L0_attn_Wq"), (wqkv[:, D:2 * D], "L0_attn_Wk"), (wqkv[:, 2 * D:3 * D], "L0_attn_Wv"),
                  (wo, "L0_attn_Wo")]
        ROWS_BCAST = [(bqkv[:, 0:D], "L0_attn_bq"), (bqkv[:, D:2 * D], "L0_attn_bk"),
                      (bqkv[:, 2 * D:3 * D], "L0_attn_bv"), (bo[:], "L0_attn_bo"), (fcb[:], "L0_xattn_fc_b")]
        LATE = [(fcw, "fc_wT"), (rw, "router_wT"), (sg, "shared_gateT"), (su, "shared_upT"), (sd, "shared_downT")]

        def ap_of(a):
            return a if isinstance(a, bass.AP) else a[:]

        def sp_phase0(sp):
            sp.dma_start(xs[:, 0:JP], x_seq(0)).then_inc(x_in[0], 16)
            for dst, name in CONSTS:
                sp.dma_start(ap_of(dst), t[name]).then_inc(s["const_in"], 16)
            for dst, name in ROWS_BCAST:
                sp.dma_start(dst, t[name].rearrange("(o f) -> o f", o=1).broadcast_to([P, D])).then_inc(s["const_in"], 16)
        N_CONST = 16 * (len(CONSTS) + len(ROWS_BCAST))

        def dve_phase0(v):
            v.memset(eps[:], LN_EPS)
            v.memset(ones_b[:], 1.0)
            v.memset(vals[:], 1.0).then_inc(s["set"], 1)
            v.wait_ge(s["const_in"], N_CONST)
            v.tensor_copy(ident_b[:], ident[:]).then_inc(s["cast"], 1)
            v.tensor_copy(before[:], before_f[:]).then_inc(s["cast"], 1)
            v.tensor_tensor(map_w[:], map_w[:], signs[:], ALU.mult).then_inc(s["map_ready"], 1)
            v.tensor_tensor(map_b[:, 1:2], map_b[:, 0:1], signcol[:], ALU.mult).then_inc(s["map_ready"], 1)
            v.wait_ge(s["esc"], 1)
            v.tensor_scalar(inv_scale[:, 1:2], inv_scale[:, 0:1], 1.0, None, ALU.add).then_inc(s["esc_dve"], 1)
            v.wait_ge(s["esc_dve"], 1)
            v.reciprocal(inv_scale[:, 2:3], inv_scale[:, 1:2]).then_inc(s["esc_dve"], 1)

        def act_phase0(a):
            a.wait_ge(s["const_in"], N_CONST)
            a.activation(inv_scale[:, 0:1], m_col[:], ACT.Exp, scale=-1.0).then_inc(s["esc"], 1)
            a.wait_ge(s["esc_dve"], 2)
            a.activation(inv_scale[:, 3:4], inv_scale[:, 2:3], ACT.Exp, scale=-math.log(float(S))).then_inc(s["inv_ready"], 1)

        def x_seq(g):
            return t["x"][bass.ds(g * JP, JP)].rearrange("b p f -> p b f")

        qkv = [sb(f"qkv{i}", [P, JP, 3 * D]) for i in range(2)]
        ctx_s = [sb(f"ctx{i}", [KEYS, JP, D]) for i in range(2)]
        early = arena("early", 32768)
        sb1 = early()
        ln_stats = [sb1(f"ln_stats{k}", [P, JP, 6]) for k in range(2)]
        ln_mv = [sb1(f"ln_mv{k}", [P, JP, 2]) for k in range(2)]
        ln_std = [sb1(f"ln_std{k}", [P, JP]) for k in range(2)]
        ln_rstd = [sb1(f"ln_rstd{k}", [P, JP]) for k in range(2)]
        ln_bias = [sb1(f"ln_bias{k}", [P, JP]) for k in range(2)]
        xnT = [sb1(f"xnT{i}", [P, GT]) for i in range(2)]
        sq = sb1("sq", [P, JP, 2 * D])
        ss = sb1("ss", [P, JP * 2 * HEADS])
        nrm = sb1("nrm", [P, JP * 2 * HEADS])
        rn = sb1("rn", [P, JP * 2 * HEADS])
        qT = sb1("qT", [P, GT])
        mt = sb1("mt", [P, GT])
        mw = sb1("mw", [P, GT])
        xn2 = [sb1(f"xn2_{i}", [P, JP, D]) for i in range(2)]

        def sp_phase1(sp):
            sp.dma_start(seqs(xs, 1), x_seq(1)).then_inc(x_in[1], 16)
            with sp.Fori(1, NG // 2) as g2:
                for par in range(2):
                    sp.wait_ge(x_in[par], g2 * 16)
                    sp.dma_start(seqs(xs, g2 * 2 + par), x_seq(g2 * 2 + par)).then_inc(x_in[par], 16)

        def loop1(eng, step):
            def group(g2, k):
                if isinstance(g2, int):
                    g = g2 * 2 + k
                    return (g, g % 2, g // 2) if 0 <= g < NG else None
                return (g2 * 2 + k, k % 2, g2 + k // 2)

            def at(g2, k):
                step(group(g2, k + 3), group(g2, k + 2), group(g2, k + 1), group(g2, k))
            for i in range(-3, 0):
                at(0, i)
            with eng.Fori(0, NG // 2 - 2) as g2:
                at(g2, 0)
                at(g2, 1)
            for i in range(NG - 4, NG):
                at(0, i)

        def x_of(g, j):
            return xs[:, bass.ds(g * JP + j, 1)].rearrange("p o f -> p (o f)")

        def dve_phase1(v):
            def statistics(g, k, stat, mean):
                for j in range(JP):
                    i = v.bn_stats(ln_stats[k][:, j], x_of(g, j))
                i.then_inc(s[stat], 1)
                wait_on_copy(v, s[stat], g + 1)
                for j in range(JP):
                    i = v.bn_aggr(ln_mv[k][:, j], ln_stats[k][:, j])
                i.then_inc(s[mean], 1)

            def scale_and_bias(g, k, std_s, rstd_s, bias_s):
                v.wait_ge(s[std_s], g + 1)
                v.reciprocal(ln_rstd[k][:], ln_std[k][:]).then_inc(s[rstd_s], 1)
                v.wait_ge(s[rstd_s], g + 1)
                v.scalar_tensor_tensor(out=ln_bias[k][:], in0=ln_mv[k][:, :, 0], scalar=-1.0, in1=ln_rstd[k][:],
                                       op0=ALU.mult, op1=ALU.mult).then_inc(s[bias_s], 1)

            def step(first, front, middle, back):
                if first:
                    g, par, g2 = first
                    v.wait_ge(x_in[par], g2 * 16 + 16)
                    statistics(g, 0, "stat1", "mean1")
                if middle:
                    g, par, _ = middle
                    v.wait_ge(s["sq1"], g + 1)
                    v.tensor_reduce(ss[:], sq[:].rearrange("p j (h d) -> p (j h) d", d=HD), AX.X, ALU.add).then_inc(s["ss1"], 1)
                if first:
                    scale_and_bias(first[0], 0, "std1", "rstd1", "bias1")
                if middle:
                    v.wait_ge(s["nrm1"], g + 1)
                    v.tensor_scalar(nrm[:], nrm[:], L2_EPS, None, ALU.max).then_inc(s["nmax1"], 1)
                    v.wait_ge(s["nmax1"], g + 1)
                    v.reciprocal(rn[:], nrm[:]).then_inc(s["rn1"], 1)
                if back:
                    g, par, _ = back
                    v.wait_ge(s["yp"], g + 1)
                    v.wait_ge(s["xb1"], g + 1)
                    x_g = seqs(xs, g).rearrange("p j f -> p (j f)")
                    v.tensor_tensor(x_g, bank[7][:], x_g, ALU.add).then_inc(s["x1"], 1)
                    wait_on_copy(v, s["x1"], g + 1)
                    statistics(g, 1, "stat2", "mean2")
                    scale_and_bias(g, 1, "std2", "rstd2", "bias2")
                if front:
                    g, par, _ = front
                    for j in range(JP):
                        v.wait_ge(s["qkvp"], g * JP + (j + 1))
                        v.tensor_tensor(qkv[par][:, j], bank[1 + j][:, 0:3 * D], bqkv[:], ALU.add).then_inc(s["qkv1"], 1)
                if middle:
                    g, par, _ = middle
                    v.wait_ge(s["kvp"], g + 1)
                    v.scalar_tensor_tensor(out=mt[:].rearrange("p (j f) -> p j f", j=JP),
                                           in0=bank[6][:].rearrange("p (j f) -> p j f", j=JP), scalar=inv_scale[:, 3:4],
                                           in1=headmask[:].rearrange("p (o f) -> p o f", o=1).broadcast_to([P, JP, P]),
                                           op0=ALU.mult, op1=ALU.mult).then_inc(s["mt1"], 1)
            v.wait_ge(s["inv_ready"], 1)
            loop1(v, step)

        def act_phase1(a):
            def deviation(g, k, mean, std_s):
                a.wait_ge(s[mean], g + 1)
                a.activation(ln_std[k][:], ln_mv[k][:, :, 1], ACT.Sqrt, bias=eps[:]).then_inc(s[std_s], 1)

            def normalise(g, k, bias_s, dst, done):
                a.wait_ge(s[bias_s], g + 1)
                for j in range(JP):
                    i = a.activation(dst[:, j], x_of(g, j), ACT.Identity, scale=ln_rstd[k][:, j:j + 1], bias=ln_bias[k][:, j:j + 1])
                i.then_inc(s[done], 1)

            def step(first, front, middle, back):
                if front:
                    g, par, _ = front
                    a.wait_ge(s["xT1p"], g + 1)
                    a.copy(xnT[par][:], bank[0][:]).then_inc(s["xT1"], 1)
                if middle:
                    g, par, _ = middle
                    a.wait_ge(s["qkv1"], g * JP + JP)
                    a.activation(sq[:], qkv[par][:, :, 0:2 * D], ACT.Square).then_inc(s["sq1"], 1)
                if first:
                    deviation(first[0], 0, "mean1", "std1")
                if middle:
                    a.wait_ge(s["ss1"], g + 1)
                    a.activation(nrm[:], ss[:], ACT.Sqrt).then_inc(s["nrm1"], 1)
                if first:
                    g, par, _ = first
                    normalise(g, 0, "bias1", xn[par], "xn1")
                if back:
                    g, par, _ = back
                    deviation(g, 1, "mean2", "std2")
                    normalise(g, 1, "bias2", xn2[par], "xn2")
                if middle:
                    g = middle[0]
                    a.wait_ge(s["qTp"], g + 1)
                    a.copy(qT[:], bank[5][:]).then_inc(s["qT1"], 1)
                if back:
                    g = back[0]
                    a.wait_ge(s["xT2p"], g + 1)
                    a.copy(xT[:, bass.ds(g * GT, GT)], bank[7][:]).then_inc(s["xT2"], 1)
                if middle:
                    g = middle[0]
                    a.wait_ge(s["mwp"], g + 1)
                    a.copy(mw[:], bank[6][:]).then_inc(s["mw1"], 1)
            a.wait_ge(s["set"], 1)
            loop1(a, step)

        def pool_phase1(p):
            def step(first, front, middle, back):
                if middle:
                    g, par, _ = middle
                    p.wait_ge(s["rn1"], g + 1)
                    for j in range(JP):
                        qk = qkv[par][:, j, 0:2 * D].rearrange("p (h d) -> p h d", d=HD)
                        r = rn[:, j * 2 * HEADS:(j + 1) * 2 * HEADS].rearrange("p (h o) -> p h o", o=1).broadcast_to([P, 2 * HEADS, HD])
                        p.tensor_tensor(qk, qk, r, ALU.mult).then_inc(s["qkn1"], 1)
                if first:
                    g = first[0]
                    p.wait_ge(s["xn1"], g + 1)
                    p.tensor_tensor(seqs(xs, g), seqs(xs, g),
                                    bo[:].rearrange("p (o f) -> p o f", o=1).broadcast_to([P, JP, D]), ALU.add).then_inc(s["xb1"], 1)
            p.wait_ge(s["const_in"], N_CONST)
            loop1(p, step)

        def pe_phase1(pe):
            def step(first, front, middle, back):
                if back:
                    g = back[0]
                    pe.wait_ge(s["qT1"], g + 1)
                    pe.wait_ge(s["mw1"], g + 1)
                    for j in range(JP):
                        i = pe.matmul(bank[7][:, j * P:(j + 1) * P], qT[:, j * P:(j + 1) * P], mw[:, j * P:(j + 1) * P],
                                      start=True, stop=True)
                    i.then_inc(s["yp"], 1)
                if front:
                    g, par, _ = front
                    pe.wait_ge(s["xn1"], g + 1)
                    for j in range(JP):
                        i = pe.transpose(bank[0][:, j * P:(j + 1) * P], xn[par][:, j], ident[:])
                    i.then_inc(s["xT1p"], 1)
                    pe.wait_ge(s["xT1"], g + 1)
                    if not is_first(g):
                        pe.wait_ge(s["qkv1"], g * JP)
                    for j in range(JP):
                        pe.matmul(bank[1 + j][:, 0:3 * D], xnT[par][:, j * P:(j + 1) * P], wqkv[:],
                                  start=True, stop=True).then_inc(s["qkvp"], 1)
                if middle:
                    g, par, _ = middle
                    for j in range(JP):
                        pe.wait_ge(s["qkn1"], g * JP + (j + 1))
                        i = pe.transpose(bank[5][:, j * P:(j + 1) * P], qkv[par][:, j, 0:D], ident[:])
                        if j == JP - 1:
                            i.then_inc(s["qTp"], 1)
                        i = pe.matmul(bank[6][:, j * P:(j + 1) * P], qkv[par][:, j, 2 * D:3 * D], qkv[par][:, j, D:2 * D],
                                      start=True, stop=True)
                    i.then_inc(s["kvp"], 1)
                if back:
                    g, par, _ = back
                    pe.wait_ge(s["xn2"], g + 1)
                    for j in range(JP):
                        i = pe.transpose(bank[7][:, j * P:(j + 1) * P], xn2[par][:, j], ident[:])
                    i.then_inc(s["xT2p"], 1)
                if middle:
                    g = middle[0]
                    pe.wait_ge(s["mt1"], g + 1)
                    for j in range(JP):
                        i = pe.matmul(bank[6][:, j * P:(j + 1) * P], mt[:, j * P:(j + 1) * P], wo[:], start=True, stop=True)
                    i.then_inc(s["mwp"], 1)
            pe.wait_ge(s["const_in"], N_CONST)
            loop1(pe, step)

        sb2 = early()
        ctxT = sb2("ctxT_s", [P, JK])
        qf = [[qkv[par][:].rearrange("p j f -> p (j f)")[:, hf * GT:(hf + 1) * GT] for hf in range(2)] for par in range(2)]
        kf = [[sb2(f"kf{par}_{hf}", [P, JK])[:] for hf in range(2)] for par in range(2)]
        qpart = [[sb2(f"qpart{par}_{hf}", [P, PARTS, GT], BF16) for hf in range(2)] for par in range(2)]
        kpart = [[sb2(f"kpart{par}_{hf}", [P, PARTS, JK], BF16) for hf in range(2)] for par in range(2)]
        res_q = [sb2(f"res_q{hf}", [P, GT]) for hf in range(2)]
        res_k = [sb2(f"res_k{hf}", [P, JK]) for hf in range(2)]

        def loop2(eng, body):
            for par in range(2):
                body(par, par, 0)
            with eng.Fori(1, NG // 2) as g2:
                for par in range(2):
                    body(g2 * 2 + par, par, g2)

        def sp_phase2(sp, prefetch):
            def ctx_load(g, par):
                sp.dma_start(ctx_s[par][:], t["ctx_1024"][bass.ds(g * JP, JP)].rearrange("b p f -> p b f")).then_inc(c_in[par], 16)
            for par in range(2):
                ctx_load(par, par)

            def body(g, par, g2):
                for hf in range(2):
                    heads = slice(hf * HALF, (hf + 1) * HALF)
                    sp.wait_ge(s["klo"], g * 2 + (hf + 1))
                    for a in range(PARTS):
                        sp.dma_start(kparts[a, :, heads, bass.ds(g * JK, JK)].rearrange("e h t -> h e t"),
                                     kpart[par][hf][:, a]).then_inc(k_sent[par][hf], 16)
                for hf in range(2):
                    heads = slice(hf * HALF, (hf + 1) * HALF)
                    sp.wait_ge(s["qlo"], g * 2 + (hf + 1))
                    sp.dma_start(qparts[heads, :, :, bass.ds(g * GT, GT)].rearrange("h e a t -> (h e) a t"),
                                 qpart[par][hf][:]).then_inc(q_sent[par][hf], 16)
            with sp.Fori(0, NG // 2 - 1) as g2:
                for par in range(2):
                    sp.wait_ge(s["ctxTp"], g2 * 2 + (par + 1))
                    ctx_load(g2 * 2 + par + 2, par)
                    body(g2 * 2 + par, par, g2)
            all_sent(sp, NG // 2 - 1)
            for par in range(2):
                prefetch(par)
                body(NG - 2 + par, par, NG // 2 - 1)

        def all_sent(sp, n):
            for par in range(2):
                for hf in range(2):
                    sp.wait_ge(q_sent[par][hf], n * 16)
                    sp.wait_ge(k_sent[par][hf], n * 16 * PARTS)

        def pe_phase2(pe):
            def body(g, par, g2):
                first = is_first(g)
                pe.wait_ge(c_in[par], g2 * 16 + 16)
                for j in range(JP):
                    i = pe.transpose(bank[0][:, j * KEYS:(j + 1) * KEYS], ctx_s[par][:, j], ident[0:KEYS, 0:KEYS])
                i.then_inc(s["ctxTp"], 1)
                pe.wait_ge(s["ctxT"], g + 1)
                if not first:
                    pe.wait_ge(s["khi"], g * 2)
                for hf in range(2):
                    pe.matmul(bank[1 + hf][:, 0:JK], map_w[:, hf], ctxT[:], start=True, stop=True).then_inc(s["zkp"], 1)
                if not first:
                    pe.wait_ge(s["qhi"], g * 2)
                for hf in range(2):
                    pe.matmul(bank[3 + hf][:], map_w[:, hf], xT[:, bass.ds(g * GT, GT)],
                              start=True, stop=True).then_inc(s["zqp"], 1)
                pe.wait_ge(s["kf"], g * 2 + 2)
                if not first:
                    pe.wait_ge(s["v_ready"], g * 2)
                for hf in range(2):
                    for j in range(JP):
                        i = pe.transpose(bank[5 + j // 2][0:KEYS, (j % 2) * 2 * P + hf * P:(j % 2) * 2 * P + (hf + 1) * P],
                                         kf[par][hf][:, j * KEYS:(j + 1) * KEYS], ident[:])
                i.then_inc(s["vp"], 1)
            pe.wait_ge(s["xT2"], NG)
            loop2(pe, body)

        def act_phase2(a):
            def features(g, par, g2, hf, z, f, part, zp, f_done, hi_done, lo, sent, loads):
                a.wait_ge(s[zp], g * 2 + (hf + 1))
                if not (isinstance(g, int) and g < 2):
                    a.wait_ge(s[lo], g * 2 + (hf - 3))
                a.activation(f, z, ACT.Exp, bias=map_b[:, 1:2]).then_inc(s[f_done], 1)
                if not (isinstance(g, int) and g < 2):
                    a.wait_ge(sent, g2 * (16 * loads))
                a.activation(part[:, 0], z, ACT.Exp, bias=map_b[:, 1:2]).then_inc(s[hi_done], 1)

            def body(g, par, g2):
                a.wait_ge(s["ctxTp"], g + 1)
                a.copy(ctxT[:], bank[0][:, 0:JK]).then_inc(s["ctxT"], 1)
                for hf in range(2):
                    features(g, par, g2, hf, bank[1 + hf][:, 0:JK], kf[par][hf], kpart[par][hf],
                             "zkp", "kf", "khi", "klo", k_sent[par][hf], PARTS)
                for hf in range(2):
                    features(g, par, g2, hf, bank[3 + hf][:], qf[par][hf], qpart[par][hf],
                             "zqp", "qf", "qhi", "qlo", q_sent[par][hf], 1)
                a.wait_ge(s["vp"], g + 1)
                for jj in range(2):
                    a.copy(vals[:, bass.ds(g * JP + 2 * jj, 2), :, 0:EX],
                           bank[5 + jj][0:KEYS].rearrange("p (j h e) -> p j h e", j=2, e=EX)).then_inc(s["v_ready"], 1)
            a.wait_ge(s["map_ready"], 2)
            loop2(a, body)

        def dve_phase2(v):
            def body(g, par, g2):
                if not is_first(g):
                    v.wait_ge(s["qlo"], g * 2)
                for hf in range(2):
                    v.wait_ge(s["qhi"], g * 2 + (hf + 1))
                    v.tensor_tensor(res_q[hf][:], qf[par][hf], qpart[par][hf][:, 0], ALU.subtract).then_inc(s["qres"], 1)
                for hf in range(2):
                    v.wait_ge(s["qres"], g * 2 + (hf + 1))
                    v.tensor_copy(qpart[par][hf][:, 1], res_q[hf][:]).then_inc(s["qmid"], 1)
                for hf in range(2):
                    v.wait_ge(s["qmid"], g * 2 + (hf + 1))
                    v.tensor_tensor(qpart[par][hf][:, 2], res_q[hf][:], qpart[par][hf][:, 1], ALU.subtract).then_inc(s["qlo"], 1)
            loop2(v, body)

        def pool_phase2(p):
            def body(g, par, g2):
                if not is_first(g):
                    p.wait_ge(s["klo"], g * 2)
                for hf in range(2):
                    p.wait_ge(s["khi"], g * 2 + (hf + 1))
                    p.tensor_tensor(res_k[hf][:], kf[par][hf], kpart[par][hf][:, 0], ALU.subtract).then_inc(s["kres"], 1)
                for hf in range(2):
                    p.wait_ge(s["kres"], g * 2 + (hf + 1))
                    p.tensor_tensor(kpart[par][hf][:, 1], res_k[hf][:], eps_p[:].broadcast_to([P, JK]), ALU.add).then_inc(s["kmid"], 1)
                for hf in range(2):
                    p.wait_ge(s["kmid"], g * 2 + (hf + 1))
                    p.tensor_tensor(kpart[par][hf][:, 2], res_k[hf][:], kpart[par][hf][:, 1], ALU.subtract).then_inc(s["klo"], 1)
            p.wait_ge(s["filled"], 16)
            p.memset(mpart[:], 0.0).then_inc(s["ones_rows"], 1)
            for k in range(NBUF):
                p.wait_ge(s["ones_rows"], k + 1)
                p.memset(kst[k][ROWS:SHIFT_ROWS], 1.0).then_inc(s["ones_rows"], 1)
            p.wait_ge(s["ones_rows"], 1 + NBUF)
            loop2(p, body)

        late = arena("late", 72704)
        sb3 = late()
        qst = [sb3(f"qst{i}", [SHIFT_ROWS, HEADS, JA * S], BF16) for i in range(NBUF)]
        kst = [sb3(f"kst{i}", [SHIFT_ROWS, HEADS, JA * KEYS], BF16) for i in range(NBUF)]
        mx = sb3("mx", [P, JA, HEADS])
        mres = sb3("mres_s", [P, JA, HEADS])
        mpart = sb3("mpart", [P, JA, PARTS + 1, HEADS], BF16)
        mT = [sb3(f"mT{i}", [P, S], BF16) for i in range(2)]
        prob = [sb3(f"prob{i}", [KEYS, 4, S]) for i in range(2)]
        avs = sb3("avs_s", [P, 512])
        rden = sb3("rden_s", [P, HEADS])
        avn = sb3("avn_s", [P, HEADS, EX])
        avnT = sb3("avnT", [P, 2 * P])
        vcur = [sb3(f"vcur{i}", [KEYS, HEADS, EX + 1]) for i in range(2 * JA)]

        LOADS = 16 * (len(Q_PART) + len(K_RUNS))

        def loop3(eng, body, step_a):
            step_a(0, 0, 0)
            step_a(1, 1, 0)
            body(0, 0, 0)
            with eng.Fori(0, NA // NBUF - 1) as g4:
                for r in range(NBUF):
                    body(g4 * NBUF + (r + 1), (r + 1) % NBUF, g4 + (r + 1) // NBUF)
            for g in range(NA - NBUF + 1, NA):
                body(g, g % NBUF, g // NBUF)

        def is_last(g, n=0):
            return isinstance(g, int) and g >= NA - n

        def load_parts(sp, g, r):
            for at, part, n in Q_RUNS:
                for i in range(n):
                    sp.dma_start(qst[r][(at + i) * EX:(at + i + 1) * EX],
                                 qparts[:, :, part, bass.ds(g * JA * S, JA * S)].rearrange("h e t -> e h t")).then_inc(parts_in[r], 16)
            for at, part, n in K_RUNS:
                sp.dma_start(kst[r][at * EX:(at + n) * EX],
                             kparts[part:part + n, :, :, bass.ds(g * JA * KEYS, JA * KEYS)].rearrange("a e h t -> (a e) h t")).then_inc(parts_in[r], 16)

        def sp_phase3(sp):
            def shift(g, r):
                sp.wait_ge(s["mT"], g + 1)
                for j in range(JA):
                    at = j * (PARTS + 1) * HEADS
                    sp.dma_start(qst[r][ROWS:SHIFT_ROWS, :, j * S:(j + 1) * S], mT[r % 2][at:at + PARTS * HEADS]).then_inc(m_in[r], 16)

            def step_a(g, r, gb):
                if g == 0:
                    shift(g, r)
                    load_parts(sp, 2, 2)
                    all_sent(sp, NG // 2)

            def body(g, r, gb):
                if not is_last(g, 3):
                    if not (is_first(g)):
                        sp.wait_ge(s["bp"], g * (4 * JA))
                    load_parts(sp, g + 3, (r + 3) % NBUF)
                if not is_last(g, 1):
                    shift(g + 1, (r + 1) % NBUF)
            loop3(sp, body, step_a)

        def pe_phase3(pe):
            def scores(g, r, j, u):
                h0, h1 = UNITS[u]
                n = j * len(UNITS) + u
                if not (is_first(g) and n < 2):
                    pe.wait_ge(s["amax"], g * (len(UNITS) * JA) + (n - 1))
                for h in range(h0, h1):
                    i = pe.matmul(bank[n % 2][:, (h - h0) * KEYS:(h - h0 + 1) * KEYS],
                                  qst[r][0:ROWS, h, j * S:(j + 1) * S], kst[r][0:ROWS, h, j * KEYS:(j + 1) * KEYS],
                                  start=True, stop=True)
                i.then_inc(s["ap"], 1)

            def turn_shift(g):
                if not is_first(g):
                    pe.wait_ge(s["mT"], g)
                pe.wait_ge(s["mlo"], g + 1)
                pe.transpose(bank[5][:, 256:256 + S // 2].bitcast(BF16), mpart[:].rearrange("p j a h -> p (j a h)"),
                             ident_b[:]).then_inc(s["mTp"], 1)

            def step_a(g, r, gb):
                pe.wait_ge(parts_in[r], gb * LOADS + LOADS)
                for j in range(JA):
                    for u in range(len(UNITS)):
                        scores(g, r, j, u)
                if g == 0:
                    turn_shift(g)

            def attend(g, r, j, tails, ahead):
                for u in range(5):
                    if u < 4:
                        n = j * 4 + u
                        if not (is_first(g) and n < 2):
                            pe.wait_ge(s["expd"], g * (4 * JA) + (n - 1))
                        for c in range(4):
                            h = 4 * u + c
                            i = pe.matmul(bank[2 + u % 2][0:KEYS, c * S:(c + 1) * S],
                                          kst[r][0:SHIFT_ROWS, h, j * KEYS:(j + 1) * KEYS],
                                          qst[r][0:SHIFT_ROWS, h, j * S:(j + 1) * S], start=True, stop=True)
                        i.then_inc(s["bp"], 1)
                    ahead(u)
                    if u == 1 and tails:
                        tails[0]()
                    if u > 0:
                        n = j * 4 + u - 1
                        pe.wait_ge(s["expd"], g * (4 * JA) + (n + 1))
                        if u == 1:
                            pe.wait_ge(s["v_cur"], g * JA + (j + 1))
                        if u == 1 and not (is_first(g) and j == 0):
                            pe.wait_ge(s["avs"], g * JA + j)
                        for c in range(4):
                            i = pe.matmul(bank[4][32 * c:32 * c + EX + 1, (u - 1) * P:u * P],
                                          av_lhs(g, r, j, 4 * (u - 1) + c), prob[(u - 1) % 2][:, c],
                                          start=True, stop=True)
                        i.then_inc(s["avp"], 1)
                    if u == 2 and tails:
                        tails[1]()
                    if u == 4 and tails:
                        tails[2]()

            def av_lhs(g, r, j, h):
                return vcur[(r % 2) * JA + j][:, h]

            def tail(g, j):
                def t1():
                    pe.wait_ge(s["avs"], g * JA + (j + 1))
                    for u in range(4):
                        i = pe.transpose(bank[6][:, u * P:(u + 1) * P], avs[:, u * P:(u + 1) * P], ident[:])
                    i.then_inc(s["tavp"], 1)

                def t2():
                    pe.wait_ge(s["avn"], g * JA + (j + 1))
                    for k in range(2):
                        i = pe.transpose(bank[7][:, k * P:(k + 1) * P], avn[:, k * HALF:(k + 1) * HALF].rearrange("p h e -> p (h e)"), ident[:])
                    i.then_inc(s["t2p"], 1)

                def t3():
                    pe.wait_ge(s["t2"], g * JA + (j + 1))
                    for k in range(2):
                        i = pe.matmul(bank[5][:, 0:D], avnT[:, k * P:(k + 1) * P], fcw[:, k], start=(k == 0), stop=(k == 1))
                    i.then_inc(s["fcp"], 1)
                return [t1, t2, t3]

            def body(g, r, gb):
                pe.wait_ge(m_in[r], gb * (16 * JA) + 16 * JA)
                first = is_first(g)
                more = not is_last(g, 2)
                rn_, gn = (r + 2) % NBUF, (gb if r < 2 else gb + 1)

                def ahead(j):
                    def f(u):
                        if j == 0 and u == 0 and more:
                            pe.wait_ge(parts_in[rn_], gn * LOADS + LOADS)
                        if j == 0 and u == 3 and not is_last(g, 1):
                            turn_shift(g + 1)
                        if more and u < len(UNITS):
                            scores(g + 2, rn_, j, u)
                    return f
                attend(g, r, 0, [] if first else tail(g - 1, 1), ahead(0))
                attend(g, r, 1, tail(g, 0), ahead(1))
            pe.wait_ge(s["ones_rows"], 1 + NBUF)
            pe.wait_ge(s["weights_in"], 16 * len(LATE))
            pe.wait_ge(s["v_ready"], 2 * NG)
            loop3(pe, body, step_a)
            for f in tail(NA - 1, 1):
                f()


        def dve_phase3(v):
            def step_a(g, r, gb):
                for n in range(3 * JA):
                    maxima(g, n)
                parts(g)

            def maxima(g, n):
                h0, h1 = UNITS[n % 3]
                v.wait_ge(s["ap"], g * (3 * JA) + (n + 1))
                v.tensor_reduce(mx[:, n // 3, h0:h1], bank[n % 2][:, 0:(h1 - h0) * KEYS].rearrange("p (h k) -> p h k", k=KEYS),
                                AX.X, ALU.max).then_inc(s["amax"], 1)

            def parts(g):
                v.wait_ge(s["amax"], g * (3 * JA) + 3 * JA)
                v.tensor_scalar(mx[:], mx[:], -1.0, None, ALU.mult).then_inc(s["neg"], 1)
                v.wait_ge(s["neg"], g + 1)
                v.tensor_copy(mpart[:, :, 0], mx[:]).then_inc(s["mhi"], 1)
                v.wait_ge(s["mhi"], g + 1)
                v.tensor_tensor(mres[:], mx[:], mpart[:, :, 0], ALU.subtract).then_inc(s["mres"], 1)
                v.wait_ge(s["mres"], g + 1)
                v.tensor_copy(mpart[:, :, 1], mres[:]).then_inc(s["mmid"], 1)
                v.wait_ge(s["mmid"], g + 1)
                v.tensor_tensor(mpart[:, :, 2], mres[:], mpart[:, :, 1], ALU.subtract).then_inc(s["mlo"], 1)

            def tail(g, j, stage):
                b = g * JA + j
                if stage == 1:
                    v.wait_ge(s["tavp"], b + 1)
                    av = bank[6][:].rearrange("p (h w) -> p h w", w=32)
                    v.reciprocal(rden[:], av[:, :, EX:EX + 1].rearrange("p h o -> p (h o)")).then_inc(s["rden"], 1)
                    v.wait_ge(s["rden"], b + 1)
                    v.tensor_tensor(avn[:], av[:, :, 0:EX], rden[:].rearrange("p (h o) -> p h o", o=1).broadcast_to([P, HEADS, EX]),
                                    ALU.mult).then_inc(s["avn"], 1)
                if stage == 2:
                    if is_first(g) and j == 0:
                        v.wait_ge(s["xb2"], 1)
                    v.wait_ge(s["fcp"], b + 1)
                    x_b = xs[:, bass.ds(b, 1)].rearrange("p o f -> p (o f)")
                    v.tensor_tensor(x_b, bank[5][:, 0:D], x_b, ALU.add).then_inc(s["x2"], 1)
                    wait_on_copy(v, s["x2"], b + 1)
                    v.bn_stats(stats3[:, bass.ds(b, 1)].rearrange("p o f -> p (o f)"), x_b).then_inc(s["stat3"], 1)

            def body(g, r, gb):
                first = is_first(g)
                more = not is_last(g, 2)
                for j in range(JA):
                    back = None if (first and j == 0) else ((g - 1, 1) if j == 0 else (g, 0))
                    if more:
                        maxima(g + 2, j * 3)
                        maxima(g + 2, j * 3 + 1)
                    if back:
                        tail(*back, 1)
                    if more:
                        maxima(g + 2, j * 3 + 2)
                    v.wait_ge(s["avp"], g * (4 * JA) + (4 * j + 4))
                    v.tensor_copy(avs[:], bank[4][:]).then_inc(s["avs"], 1)
                    if back:
                        tail(*back, 2)
                if more:
                    parts(g + 2)
            v.wait_ge(s["ones_rows"], 1)
            loop3(v, body, step_a)
            tail(NA - 1, 1, 1)
            tail(NA - 1, 1, 2)

        def act_phase3(a):
            def copy_shift(g, r):
                a.wait_ge(s["mTp"], g + 1)
                a.copy(mT[r % 2][:], bank[5][:, 256:256 + S // 2].bitcast(BF16)).then_inc(s["mT"], 1)

            def step_a(g, r, gb):
                if g == 0:
                    copy_shift(g, r)

            def body(g, r, gb):
                first = is_first(g)
                for j in range(JA):
                    back = None if (first and j == 0) else (g * JA + j - 1)
                    for u in range(4):
                        n = j * 4 + u
                        a.wait_ge(s["bp"], g * (4 * JA) + (n + 1))
                        if not (first and n < 2):
                            a.wait_ge(s["avp"], g * (4 * JA) + (n - 1))
                        a.activation(prob[u % 2][:].rearrange("p c t -> p (c t)"), bank[2 + u % 2][0:KEYS], ACT.Exp,
                                     scale=SCORE_SCALE).then_inc(s["expd"], 1)
                        if j == 0 and u == 2 and not is_last(g, 1):
                            copy_shift(g + 1, (r + 1) % NBUF)
                        if u == 3 and back is not None:
                            a.wait_ge(s["t2p"], back + 1)
                            a.copy(avnT[:], bank[7][:, 0:2 * P]).then_inc(s["t2"], 1)
            loop3(a, body, step_a)
            a.wait_ge(s["t2p"], B)
            a.copy(avnT[:], bank[7][:, 0:2 * P]).then_inc(s["t2"], 1)


        def pool_phase3(p):
            p.wait_ge(s["v_ready"], 2 * NG)

            def copy_values(b, k):
                p.tensor_copy(vcur[k][:], vals[:, bass.ds(b, 1)].rearrange("p o h e -> p (o h) e")).then_inc(s["v_cur"], 1)
            for b in range(2 * JA):
                copy_values(b, b)
            p.wait_ge(s["xn2"], NG)
            p.tensor_tensor(xs[:], xs[:], fcb[:].rearrange("p (o f) -> p o f", o=1).broadcast_to([P, B, D]),
                            ALU.add).then_inc(s["xb2"], 1)
            with p.Fori(1, B // (2 * JA)) as i:
                for k in range(2 * JA):
                    p.wait_ge(s["avp"], i * (4 * 2 * JA) + (4 * (k + 1) - 4 * 2 * JA))
                    copy_values(i * (2 * JA) + k, k)

        sb4 = late()
        N_LG = B * EXPERTS
        h_rows = sb4("h_rows", [P, B, ROW])
        lgT = [sb4(f"lgT{i}", [EXPERTS, GT]) for i in range(2)]
        lg = sb4("lg_s", [P, N_LG])
        best = sb4("best", [P, B])
        wrk = sb4("wrk", [P, N_LG])
        low = sb4("low", [P, B])
        oh = sb4("oh_s", [P, N_LG])
        oh_b = sb4("oh_b", [P, N_LG], BF16)
        tot = sb4("tot", [P, N_LG])
        cum = sb4("cum", [P, N_LG])
        onesf = sb4("onesf", [P, N_LG])
        cnt = sb4("cnt", [P, EXPERTS])
        cnt_i = sb4("cnt_i", [P, EXPERTS], I32)
        tiles_f = sb4("tiles_f", [P, EXPERTS])
        tile_end = sb4("tile_end", [P, EXPERTS])
        adj = sb4("adj", [P, EXPERTS])
        esc = sb4("esc_s", [P, B])
        score = sb4("score_s", [P, B])
        posf = sb4("posf", [P, B])
        pos = sb4("pos_s", [P, B], I32)
        owner_w = sb4("owner_w", [P, TILES, EXPERTS])
        owner_f = sb4("owner_f", [P, TILES])
        owner = sb4("owner", [P, TILES], I32)
        s_g = [sb4(f"s_g{i}", [P, GT]) for i in range(2)]
        act = [sb4(f"act{i}", [P, GT]) for i in range(CH)]
        sb5 = early()
        t_row = [sb5(f"t_row{i}", [P, ROW]) for i in range(RING)]
        t_w = [sb5(f"t_w{i}", [P, FF3]) for i in range(RING)]
        t_hT = [sb5(f"t_hT{i}", [P, P]) for i in range(2)]
        t_sg = [sb5(f"t_sg{i}", [P, P]) for i in range(2)]
        t_act = [sb5(f"t_act{i}", [P, P]) for i in range(2)]
        t_no = [sb5(f"t_no{i}", [P, 1], I32) for i in range(RING)]
        t_y = [sb5(f"t_y{i}", [P, D]) for i in range(RING)]
        y_back = [sb4(f"y_back{i}", [P, JP, D]) for i in range(2)]

        def bc(ap, n):
            return ap.rearrange("p (m o) -> p m o", o=1).broadcast_to([P, ap.shape[1], n])

        def rep(ap, n):
            return ap.rearrange("p (o m) -> p o m", o=1).broadcast_to([P, n, ap.shape[1]])

        def dve_phase4(v):
            def step(i):
                steps[0] += 1
                i.then_inc(s["r_step"], 1)
                v.wait_ge(s["r_step"], steps[0])
            steps = [0]

            def gated(g, c):
                v.wait_ge(s["silu"], g * CH + (c + 1))
                v.tensor_tensor(act[c][:], bank[BK_UP[c % 2]][:], s_g[c % 2][:], ALU.mult).then_inc(s["act"], 1)

            def add_down(g, par):
                v.wait_ge(s["downp"], g + 1)
                x_g = seqs(xs, g).rearrange("p j f -> p (j f)")
                v.tensor_tensor(x_g, bank[BK_DOWN[par]][:], x_g, ALU.add).then_inc(s["x3"], 1)

            v.wait_ge(s["stat3"], B)
            for b in range(B):
                i = v.bn_aggr(mv[:, b], stats3[:, b])
            i.then_inc(s["mean3"], 1)
            v.wait_ge(s["std3"], 1)
            step(v.reciprocal(rstd[:], std[:]))
            for g in range(NG):
                if g >= 2:
                    v.wait_ge(s["hTp"], g - 1)
                    v.wait_ge(s["h_kept"], g - 1)
                for j in range(JP):
                    b = g * JP + j
                    i = v.tensor_scalar(xn[g % 2][:, j], xs[:, b], mv[:, b, 0:1], rstd[:, b:b + 1], ALU.subtract, ALU.mult)
                i.then_inc(s["xn3"], 1)
            v.wait_ge(s["lgtp"], NG)
            step(v.tensor_copy(lg[:], bank[BK_LG][:]))
            lg3 = lg[:].rearrange("p (b n) -> p b n", n=EXPERTS)
            wrk3 = wrk[:].rearrange("p (b n) -> p b n", n=EXPERTS)
            oh3 = oh[:].rearrange("p (b n) -> p b n", n=EXPERTS)
            v.memset(onesf[:], 1.0)
            step(v.tensor_reduce(best[:], lg3, AX.X, ALU.max))
            v.tensor_copy(esc[:], best[:]).then_inc(s["lg"], 1)
            step(v.tensor_tensor(wrk3, lg3, bc(best[:], EXPERTS), ALU.is_equal))
            step(v.scalar_tensor_tensor(out=wrk3, in0=wrk3, scalar=-float(EXPERTS), in1=rep(expert_no[:], B),
                                        op0=ALU.mult, op1=ALU.add))
            step(v.tensor_reduce(low[:], wrk3, AX.X, ALU.min))
            step(v.tensor_tensor(oh3, wrk3, bc(low[:], EXPERTS), ALU.is_equal))
            v.tensor_copy(oh_b[:], oh[:]).then_inc(s["oh"], 1)
            gated(0, 0)
            v.wait_ge(s["escore"], 1)
            step(v.tensor_scalar(esc[:], score[:], 1.0, None, ALU.add))
            v.reciprocal(posf[:], esc[:]).then_inc(s["sc_ready"], 1)
            gated(0, 1)
            v.wait_ge(s["rankp"], 1)
            tot3 = tot[:].rearrange("p (n b) -> p n b", b=B)
            cum3 = cum[:].rearrange("p (n b) -> p n b", b=B)
            step(v.tensor_copy(tot3, bank[BK_COUNT][:].rearrange("p (b n) -> p n b", n=EXPERTS)))
            step(v.tensor_tensor_scan(out=cum[:], data0=onesf[:], data1=tot[:], initial=0.0, op0=ALU.mult, op1=ALU.add))
            step(v.tensor_tensor(tot[:], cum[:], tot[:], ALU.subtract))
            gated(0, 2)
            first, last = tot3[:, :, 0], cum3[:, :, B - 1]
            step(v.tensor_tensor(cnt[:], last, first, ALU.subtract))
            step(v.tensor_scalar(cnt[:], cnt[:], float(P - 1), None, ALU.add))
            step(v.tensor_copy(cnt_i[:], cnt[:]))
            step(v.tensor_scalar(cnt_i[:], cnt_i[:], 7, None, ALU.logical_shift_right))
            step(v.tensor_copy(tiles_f[:], cnt_i[:]))
            step(v.tensor_tensor_scan(out=tile_end[:], data0=onesf[:, 0:EXPERTS], data1=tiles_f[:], initial=0.0,
                                      op0=ALU.mult, op1=ALU.add))
            step(v.tensor_tensor(adj[:], tile_end[:], tiles_f[:], ALU.subtract))
            step(v.scalar_tensor_tensor(out=adj[:], in0=adj[:], scalar=float(P), in1=first, op0=ALU.mult, op1=ALU.subtract))
            gated(0, 3)
            step(v.tensor_tensor(tot3, tot3, bc(adj[:], B), ALU.add))
            step(v.tensor_tensor(wrk3, bank[BK_RANK][:].rearrange("p (b n) -> p b n", n=EXPERTS),
                                 tot[:].rearrange("p (n b) -> p b n", b=B), ALU.add))
            step(v.tensor_tensor(wrk[:], wrk[:], oh[:], ALU.mult))
            step(v.tensor_reduce(low[:], wrk3, AX.X, ALU.add))
            v.tensor_copy(pos[:], low[:]).then_inc(s["pos"], 1)
            gated(1, 0)
            step(v.tensor_tensor(owner_w[:], rep(tile_end[:], TILES), bc(tile_no[:], EXPERTS), ALU.is_le))
            step(v.tensor_reduce(owner_f[:], owner_w[:], AX.X, ALU.add))
            step(v.tensor_scalar(owner_f[:], owner_f[:], float(EXPERTS - 1), None, ALU.min))
            v.tensor_copy(owner[:], owner_f[:]).then_inc(s["etile"], 1)

            for c in range(1, CH):
                gated(1, c)
                if c == 1:
                    add_down(0, 0)
            with v.Fori(1, NG // 2) as g2:
                for k in range(2):
                    for c in range(CH):
                        gated(g2 * 2 + k, c)
                        if c == 1:
                            add_down(g2 * 2 + (k - 1), 1 - k)
            add_down(NG - 1, 1)

            def mul(n, r):
                v.wait_ge(s["tsilu"], n + 1)
                v.tensor_tensor(t_act[r % 2][:], bank[2 + r % 2][:, P:2 * P], t_sg[r % 2][:], ALU.mult).then_inc(s["tact"], 1)

            def leave(n, r, k):
                v.wait_ge(s["tyd"], n + 1)
                if not (isinstance(n, int) and n < RING):
                    v.wait_ge(t_out[r], k * 16)
                v.tensor_copy(t_no[r][:], t_row[r][:, D:D + 1].bitcast(I32))
                v.tensor_copy(t_y[r][:], bank[4 + r % 2][:, 0:D]).then_inc(s["ty"], 1)

            def body(n, r, k):
                if not last_tile(n, 1):
                    mul(n + 1, (r + 1) % RING)
                leave(n, r, k)
            mul(0, 0)
            loop_tiles(v, body)

            for g in range(NG):
                v.wait_ge(y_in[g % 2], (g // 2 + 1) * 16)
                v.tensor_tensor(xs[:, g * JP:(g + 1) * JP], xs[:, g * JP:(g + 1) * JP], y_back[g % 2][:], ALU.add).then_inc(s["res_add"], 1)

        BK_GATE, BK_UP, BK_DOWN = (0, 1), (2, 7), (3, 4)
        BK_LOGITS, BK_LG = (2, 5), 6
        BK_RANK, BK_COUNT = 5, 6
        SCALED = -(-B // (2 * CH - 1))

        def loop_shared(eng, body):
            body(0, 0)
            body(1, 1)
            with eng.Fori(1, NG // 2) as g2:
                for k in range(2):
                    body(g2 * 2 + k, k)

        def last_tile(n, lead):
            return isinstance(n, int) and n >= TILES - lead

        def loop_tiles(eng, body):
            for n in range(RING):
                body(n, n, 0)
            with eng.Fori(1, TILES // RING - 1) as k:
                for r in range(RING):
                    body(k * RING + r, r, k)
            for n in range(TILES - RING, TILES):
                body(n, n % RING, n // RING)

        def act_phase4(a):
            a.wait_ge(s["mean3"], 1)
            a.activation(std[:], mv[:, :, 1], ACT.Sqrt, bias=eps[:]).then_inc(s["std3"], 1)
            for i in range(NG + 1):
                if i < NG:
                    a.wait_ge(s["hTp"], i + 1)
                    a.copy(xT[:, i * GT:(i + 1) * GT], bank[i % 2][:]).then_inc(s["hT"], 1)
                if i >= 1:
                    a.wait_ge(s["lgp"], i)
                    if i >= 3:
                        a.wait_ge(s["lgtp"], i - 2)
                    a.copy(lgT[(i - 1) % 2][:], bank[BK_LOGITS[i % 2]][0:EXPERTS]).then_inc(s["lgT"], 1)
            a.wait_ge(s["lg"], 1)
            a.activation(score[:], esc[:], ACT.Exp, scale=-1.0).then_inc(s["escore"], 1)

            def shared(g, par):
                for c in range(CH):
                    a.wait_ge(s["gup"], g * CH + (c + 1))
                    if not (is_first(g) and c < 2):
                        a.wait_ge(s["act"], g * CH + (c - 1))
                    a.activation(s_g[c % 2][:], bank[BK_GATE[c % 2]][:], ACT.Silu).then_inc(s["silu"], 1)
                    if isinstance(g, int):
                        n = g * CH + c
                        if n == 1:
                            a.wait_ge(s["sc_ready"], 1)
                            a.wait_ge(s["h_kept"], NG)
                        for b in range(max(n - 1, 0) * SCALED, min(n * SCALED, B)):
                            a.activation(h_rows[:, b, 0:D], h_rows[:, b, 0:D], ACT.Copy, scale=posf[:, b:b + 1]).then_inc(s["rows"], 1)
            loop_shared(a, shared)

            def turned(n, r):
                a.wait_ge(s["tTp"], n + 1)
                a.copy(t_hT[r % 2][:], bank[0 + r % 2][:, 0:P]).then_inc(s["tT"], 1)

            def gated(n, r):
                a.wait_ge(s["tgup"], n + 1)
                a.activation(t_sg[r % 2][:], bank[2 + r % 2][:, 0:P], ACT.Silu).then_inc(s["tsilu"], 1)

            def body(n, r, k):
                if not last_tile(n, 2):
                    turned(n + 2, (r + 2) % RING)
                if not last_tile(n, 1):
                    gated(n + 1, (r + 1) % RING)
                if not (isinstance(n, int) and n < 2) and not last_tile(n, RING - 2):
                    load_rows(n + (RING - 2), (r + RING - 2) % RING)

            def load_rows(n, r):
                if not (isinstance(n, int) and n < RING):
                    a.wait_ge(s["ty"], n - (RING - 1))
                a.dma_start(t_row[r][:], sorted_in[bass.ds(n * P, P)]).then_inc(t_in[r], 16)
            a.wait_ge(s["scat"], B * 16)
            for r in range(RING):
                load_rows(r, r)
            turned(0, 0)
            turned(1, 1)
            gated(0, 0)
            loop_tiles(a, body)

        def pool_phase4(p):
            p.wait_ge(s["x2"], B)
            p.memset(h_rows[:, :, D:ROW], 0.0).then_inc(s["rows"], 1)
            p.wait_ge(s["rows"], 1)
            p.tensor_copy(h_rows[:, :, D:D + 1].bitcast(I32).rearrange("p b o -> p (b o)"), token_no[:])
            for g in range(NG):
                p.wait_ge(s["xn3"], g + 1)
                p.tensor_copy(h_rows[:, g * JP:(g + 1) * JP, 0:D], xn[g % 2][:]).then_inc(s["h_kept"], 1)
            p.wait_ge(s["pos"], 1)
            p.wait_ge(s["rows"], 1 + B)
            p.wait_ge(s["filled"], 16)
            for b in range(B):
                p.indirect_dma_start(out=sorted_in, out_offset=bass.IndirectOffsetOnAxis(ap=pos[:, b:b + 1].bitcast(U32), axis=0),
                                     in_=h_rows[:, b], in_offset=None).then_inc(s["scat"], 16)

            def body(n, r, k):
                if not is_first(n):
                    p.wait_ge(s["carried"], n)
                p.wait_ge(s["ty"], n + 1)
                p.tensor_tensor(carrier_p[:], eps_p[:], eps_p[:], ALU.add).then_inc(s["carried"], 1)
                p.indirect_dma_start(out=routed, out_offset=bass.IndirectOffsetOnAxis(ap=t_no[r][:].bitcast(U32), axis=0),
                                     in_=t_y[r][:], in_offset=None).then_inc(t_out[r], 16)
            loop_tiles(p, body)

        def pe_phase4(pe):
            for i in range(NG + 2):
                if i < NG:
                    pe.wait_ge(s["xn3"], i + 1)
                    if i >= 2:
                        pe.wait_ge(s["hT"], i - 1)
                    for j in range(JP):
                        m = pe.transpose(bank[i % 2][:, j * P:(j + 1) * P], xn[i % 2][:, j], ident[:])
                    m.then_inc(s["hTp"], 1)
                if 1 <= i <= NG:
                    pe.wait_ge(s["hT"], i)
                    pe.matmul(bank[BK_LOGITS[i % 2]][0:EXPERTS], rw[:], xT[:, (i - 1) * GT:i * GT], start=True, stop=True).then_inc(s["lgp"], 1)
                if i >= 2:
                    pe.wait_ge(s["lgT"], i - 1)
                    for j in range(JP):
                        b = (i - 2) * JP + j
                        m = pe.transpose(bank[BK_LG][:, b * EXPERTS:(b + 1) * EXPERTS], lgT[i % 2][:, j * P:(j + 1) * P], ident[0:EXPERTS, 0:EXPERTS])
                    m.then_inc(s["lgtp"], 1)

            def down(g, par, c):
                pe.wait_ge(s["act"], g * CH + (c + 1))
                for j in range(JP):
                    i = pe.matmul(bank[BK_DOWN[par]][:, j * D:(j + 1) * D], act[c][:, j * P:(j + 1) * P], sd[:, c],
                                  start=(c == 0 and j == 0), stop=(c == CH - 1), skip_group_check=True)
                if c == CH - 1:
                    i.then_inc(s["downp"], 1)

            def shared(g, par):
                first = is_first(g)
                for c in range(CH):
                    if not (first and c < 2):
                        pe.wait_ge(s["act"], g * CH + (c - 1))
                    pe.matmul(bank[BK_GATE[c % 2]][:], sg[:, c * P:(c + 1) * P], xT[:, bass.ds(g * GT, GT)], start=True, stop=True)
                    pe.matmul(bank[BK_UP[c % 2]][:], su[:, c * P:(c + 1) * P], xT[:, bass.ds(g * GT, GT)],
                              start=True, stop=True).then_inc(s["gup"], 1)
                    if c > 0:
                        down(g, par, c - 1)
                    elif not first:
                        down(g - 1, 1 - par, CH - 1)
                    if first and c == 1:
                        pe.wait_ge(s["oh"], 1)
                        pe.matmul(bank[BK_RANK][:], before[:], oh_b[:], start=True, stop=True)
                        pe.matmul(bank[BK_COUNT][:], ones_b[:], oh_b[:], start=True, stop=True).then_inc(s["rankp"], 1)
            loop_shared(pe, shared)
            down(NG - 1, 1, CH - 1)

            def turn(n, r, k):
                pe.wait_ge(t_in[r], k * 32 + 32)
                i = pe.transpose(bank[0 + r % 2][:, 0:P], t_row[r][:, 0:D], ident[:])
                i.then_inc(s["tTp"], 1)

            def gate_up(n, r):
                pe.wait_ge(s["tT"], n + 1)
                if not (isinstance(n, int) and n < 2):
                    pe.wait_ge(s["tact"], n - 1)
                pe.matmul(bank[2 + r % 2][:, 0:P], t_w[r][:, 0:FF], t_hT[r % 2][:], start=True, stop=True)
                pe.matmul(bank[2 + r % 2][:, P:2 * P], t_w[r][:, FF:2 * FF], t_hT[r % 2][:], start=True, stop=True).then_inc(s["tgup"], 1)

            def body(n, r, k):
                if not last_tile(n, 2):
                    turn(n + 2, (r + 2) % RING, k + (r + 2) // RING)
                if not last_tile(n, 1):
                    gate_up(n + 1, (r + 1) % RING)
                pe.wait_ge(s["tact"], n + 1)
                if not (isinstance(n, int) and n < 2):
                    pe.wait_ge(s["ty"], n - 1)
                pe.matmul(bank[4 + r % 2][:, 0:D], t_act[r % 2][:], t_w[r][:, 2 * FF:FF3], start=True, stop=True).then_inc(s["tyd"], 1)
            pe.wait_ge(s["x3"], NG)
            turn(0, 0, 0)
            turn(1, 1, 0)
            gate_up(0, 0)
            loop_tiles(pe, body)

        def sp_phase4(sp):
            def load_ring(n0, again):
                expert = [sp.value_load(owner[0:1, bass.ds(n0 + r, 1)], min_val=0, max_val=EXPERTS - 1) for r in range(RING)]
                for r in range(RING):
                    if again:
                        sp.wait_ge(s["tyd"], n0 + (r + 1 - RING))
                    sp.dma_start(t_w[r][:], t["expert_w"][bass.ds(expert[r], 1)].rearrange("o h f -> (o h) f")).then_inc(t_in[r], 16)
            sp.wait_ge(s["etile"], 1)
            load_ring(0, False)
            with sp.Fori(1, TILES // RING) as k:
                load_ring(k * RING, True)
            for r in range(RING):
                sp.wait_ge(t_out[r], TILES // RING * 16)
            for g in range(NG):
                if g >= 2:
                    sp.wait_ge(s["res_add"], g - 1)
                sp.dma_start(y_back[g % 2][:], routed[g * GT:(g + 1) * GT].rearrange("(j p) f -> p j f", p=P)).then_inc(y_in[g % 2], 16)
                if g >= 1:
                    store(sp, g - 1)
            store(sp, NG - 1)
            sp.wait_ge(s["res_out"], NG * 16)

        def store(sp, g):
            sp.wait_ge(s["res_add"], g + 1)
            sp.dma_start(out[g * JP:(g + 1) * JP].rearrange("b p f -> p b f"), xs[:, g * JP:(g + 1) * JP]).then_inc(s["res_out"], 16)

        fill = late()("fill", [P, TILES, ROW])

        def sp_fill(sp):
            sp.wait_ge(s["fill_set"], 2)
            sp.dma_start(sorted_in.rearrange("(p j) r -> p j r", p=P), fill[:]).then_inc(s["filled"], 16)
            for dst, name in LATE:
                sp.dma_start(ap_of(dst), t[name]).then_inc(s["weights_in"], 16)

        def pool_fill(p):
            p.memset(eps_p[:], 0.0)
            p.memset(fill[:], 0.0).then_inc(s["fill_set"], 1)
            p.wait_ge(s["const_in"], N_CONST)
            p.wait_ge(s["fill_set"], 1)
            p.tensor_copy(fill[:, :, D:D + 1].bitcast(I32).rearrange("p j o -> p (j o)"), slot_no[:]).then_inc(s["fill_set"], 1)

        block = ctx.enter_context(nc.Block())

        @block.sync
        def _(sp):
            sp_phase0(sp)
            sp_phase1(sp)
            sp_fill(sp)
            sp_phase2(sp, lambda g: load_parts(sp, g, g))
            sp_phase3(sp)
            sp_phase4(sp)

        @block.gpsimd
        def _(p):
            pool_fill(p)
            pool_phase1(p)
            pool_phase2(p)
            pool_phase3(p)
            pool_phase4(p)

        @block.tensor
        def _(pe):
            pe_phase1(pe)
            pe_phase2(pe)
            pe_phase3(pe)
            pe_phase4(pe)

        @block.vector
        def _(v):
            dve_phase0(v)
            dve_phase1(v)
            dve_phase2(v)
            dve_phase3(v)
            dve_phase4(v)

        @block.scalar
        def _(a):
            act_phase0(a)
            act_phase1(a)
            act_phase2(a)
            act_phase3(a)
            act_phase4(a)


def kernel(**inputs):
    import numpy as np
    import concourse.bacc as bacc
    from concourse.bass_utils import run_bass_kernel_spmd

    x = np.ascontiguousarray(inputs["x"])
    B, S, D = x.shape
    experts = inputs["L0_ffn_router_w"].shape[0]
    tiles = B * S // P + experts
    sf = inputs["L0_ffn_shared_gate_w"].shape[0]
    arrays = {"x": x}
    for name in ("ctx_1024", "L0_attn_Wq", "L0_attn_Wk", "L0_attn_Wv", "L0_attn_Wo", "L0_attn_bq", "L0_attn_bk",
                 "L0_attn_bv", "L0_attn_bo", "L0_xattn_fc_b"):
        arrays[name] = inputs[name]
    fm_w = np.asarray(inputs["L0_xattn_fm_w"])
    arrays["fm_wT"] = np.tile(fm_w.T, (HEADS, 2 * HALF * 2)).reshape(P, 2, P)
    arrays["fm_b"] = np.tile(np.asarray(inputs["L0_xattn_fm_b"]), HEADS).reshape(P, 1)
    arrays["m_col"] = np.repeat(np.asarray(inputs["L0_attn_m"]), HD).reshape(P, 1)
    arrays["fc_wT"] = np.asarray(inputs["L0_xattn_fc_w"]).T.reshape(2, P, D).transpose(1, 0, 2)
    arrays["expert_w"] = np.concatenate([inputs["L0_ffn_gate_up_proj"], inputs["L0_ffn_down_proj"]], axis=2)
    arrays["router_wT"] = np.asarray(inputs["L0_ffn_router_w"]).T
    arrays["shared_gateT"] = np.asarray(inputs["L0_ffn_shared_gate_w"]).T
    arrays["shared_upT"] = np.asarray(inputs["L0_ffn_shared_up_w"]).T
    arrays["shared_downT"] = np.asarray(inputs["L0_ffn_shared_down_w"]).T.reshape(sf // P, P, D).transpose(1, 0, 2)
    r = np.arange(P)
    f32 = np.float32
    arrays["ident"] = np.eye(P, dtype=f32)
    arrays["headmask"] = (r[:, None] // HD == r[None, :] // HD).astype(f32)
    sign = np.where(r % EX < HD, 1, -1)
    arrays["signs"] = np.stack([np.where(r[:, None] // HD == hf * HALF + r[None, :] // EX, sign[None, :], 0)
                                for hf in range(2)], axis=1).astype(f32)
    arrays["signcol"] = sign.astype(f32).reshape(P, 1)
    arrays["before"] = (r[:, None] < r[None, :]).astype(f32)
    arrays["expert_no"] = np.tile(np.arange(experts, dtype=f32), (P, 1))
    arrays["tile_no"] = np.tile(np.arange(tiles, dtype=f32), (P, 1))
    arrays["token_no"] = (np.arange(B)[None, :] * P + r[:, None]).astype(np.int32)
    arrays["slot_no"] = (B * S + np.arange(P * tiles).reshape(P, tiles)).astype(np.int32)

    nc = bacc.Bacc("TRN2", target_bir_lowering=False, num_devices=1)
    feed, t = {}, {}
    for name, a in arrays.items():
        a = np.ascontiguousarray(a)
        feed[f"in_{name}"] = a
        t[name] = nc.dram_tensor(f"in_{name}", a.shape, mybir.dt.from_np(a.dtype), kind="ExternalInput").ap()
    out = nc.dram_tensor("out_x", (B, S, D), F32, kind="ExternalOutput").ap()
    decoder_layer(nc, t, out)
    r = run_bass_kernel_spmd(nc, [feed], core_ids=[0])
    return r.results[0]["out_x"]
```
